# Optimizing a Trainium2 kernel written in Bass

```python
import numpy as np
import jax
import jax.numpy as jnp

def _softmax(x, axis=-1):
    return jax.nn.softmax(x, axis=axis)

def _gelu(x):
    return jax.nn.gelu(x, approximate=True)

def _silu(x):
    return jax.nn.silu(x)

def _sigmoid(x):
    return jax.nn.sigmoid(x)

def _layernorm(x, axis=-1, eps=1e-05):
    m = jnp.mean(x, axis=axis, keepdims=True)
    v = jnp.var(x, axis=axis, keepdims=True)
    return (x - m) / jnp.sqrt(v + eps)

def _scatter_add(tgt, idx, src, axis=0):
    return tgt.at[idx].add(src)

def _segment_sum(src, seg, n):
    return jax.ops.segment_sum(src, seg, n)
kernel_name = 'mk_prb_d1_jaxref_r4_88d2cc'

def setup_inputs(seed: int=0):
    np.random.seed(seed)
    _w = jnp.asarray

    def _L0_attn_setup():
        import jax, jax.numpy as jnp
        import numpy as np
        NUM_HEADS = 16
        EPS = float(jnp.finfo(jnp.float32).eps)

        def rms_norm(x, w):
            ms = jnp.mean(x * x, axis=-1, keepdims=True)
            return x * jax.lax.rsqrt(ms + EPS) * w
        key = jax.random.key(seed)
        k = jax.random.split(key, 5)
        B, N, D = (4, 512, 256)
        Dh = D // NUM_HEADS
        return {'x': jax.random.normal(k[0], (B, N, D), dtype=jnp.float32), 'Wq': jax.random.normal(k[1], (D, D), dtype=jnp.float32) * 0.02, 'Wk': jax.random.normal(k[2], (D, D), dtype=jnp.float32) * 0.02, 'Wv': jax.random.normal(k[3], (D, D), dtype=jnp.float32) * 0.02, 'Wo': jax.random.normal(k[4], (D, D), dtype=jnp.float32) * 0.02, 'qn_w': jnp.ones((Dh,), dtype=jnp.float32), 'kn_w': jnp.ones((Dh,), dtype=jnp.float32)}
    _L0_attn_in = _L0_attn_setup()

    def _L0_ffn_setup():
        import jax, jax.numpy as jnp
        import numpy as np
        LN_EPS = 1e-05

        def layer_norm(x, g, b):
            mu = jnp.mean(x, axis=-1, keepdims=True)
            var = jnp.var(x, axis=-1, keepdims=True)
            return (x - mu) / jnp.sqrt(var + LN_EPS) * g + b

        def balanced_assignment(scores):
            T, E = scores.shape
            C = T // E
            taken = jnp.zeros((T,), dtype=bool)
            parts = []
            for e in range(E):
                s = jnp.where(taken, -jnp.inf, scores[:, e])
                _, idx = jax.lax.top_k(s, C)
                parts.append(idx)
                taken = taken.at[idx].set(True)
            return jnp.concatenate(parts)
        key = jax.random.key(seed)
        ks = jax.random.split(key, 4)
        B, S, D, F, E = (4, 512, 256, 1024, 8)
        return {'x': jax.random.normal(ks[0], (B, S, D), dtype=jnp.float32), 'centroids': jax.random.normal(ks[1], (E, D), dtype=jnp.float32) * 0.1, 'ln_g': jnp.ones((D,), dtype=jnp.float32), 'ln_b': jnp.zeros((D,), dtype=jnp.float32), 'w1': jax.random.normal(ks[2], (E, D, F), dtype=jnp.float32) * 0.02, 'b1': jnp.zeros((E, F), dtype=jnp.float32), 'w2': jax.random.normal(ks[3], (E, F, D), dtype=jnp.float32) * 0.02, 'b2': jnp.zeros((E, D), dtype=jnp.float32)}
    _L0_ffn_in = _L0_ffn_setup()
    _d = {'L0_attn_x': _L0_attn_in['x'], 'L0_attn_Wq': _L0_attn_in['Wq'], 'L0_attn_Wk': _L0_attn_in['Wk'], 'L0_attn_Wv': _L0_attn_in['Wv'], 'L0_attn_Wo': _L0_attn_in['Wo'], 'L0_attn_qn_w': _L0_attn_in['qn_w'], 'L0_attn_kn_w': _L0_attn_in['kn_w'], 'L0_ffn_centroids': _L0_ffn_in['centroids'], 'L0_ffn_ln_g': _L0_ffn_in['ln_g'], 'L0_ffn_ln_b': _L0_ffn_in['ln_b'], 'L0_ffn_w1': _L0_ffn_in['w1'], 'L0_ffn_b1': _L0_ffn_in['b1'], 'L0_ffn_w2': _L0_ffn_in['w2'], 'L0_ffn_b2': _L0_ffn_in['b2']}
    _x0 = _d['L0_attn_x']
    _d['L0_attn_x'] = jax.random.normal(jax.random.fold_in(jax.random.key(seed), 1), (16, 512, 256), dtype=_x0.dtype)
    del _x0
    return _d

def reference(L0_attn_x, L0_attn_Wq, L0_attn_Wk, L0_attn_Wv, L0_attn_Wo, L0_attn_qn_w, L0_attn_kn_w, L0_ffn_centroids, L0_ffn_ln_g, L0_ffn_ln_b, L0_ffn_w1, L0_ffn_b1, L0_ffn_w2, L0_ffn_b2):

    def _L0_attn_ref(x, Wq, Wk, Wv, Wo, qn_w, kn_w):
        import jax, jax.numpy as jnp
        import numpy as np
        NUM_HEADS = 16
        EPS = float(jnp.finfo(jnp.float32).eps)

        def rms_norm(x, w):
            ms = jnp.mean(x * x, axis=-1, keepdims=True)
            return x * jax.lax.rsqrt(ms + EPS) * w
        B, N, D = x.shape
        H = NUM_HEADS
        Dh = D // H
        scale = Dh ** (-0.5)

        def proj(W):
            return (x @ W.T).reshape(B, N, H, Dh).transpose(0, 2, 1, 3)
        q = rms_norm(proj(Wq), qn_w)
        k = rms_norm(proj(Wk), kn_w)
        v = proj(Wv)
        scores = jnp.einsum('bhnd,bhmd->bhnm', q, k) * scale
        attn = jax.nn.softmax(scores, axis=-1)
        out = jnp.einsum('bhnm,bhmd->bhnd', attn, v)
        out = out.transpose(0, 2, 1, 3).reshape(B, N, D)
        return out @ Wo.T

    def _L0_ffn_ref(x, centroids, ln_g, ln_b, w1, b1, w2, b2):
        import jax, jax.numpy as jnp
        import numpy as np
        LN_EPS = 1e-05

        def layer_norm(x, g, b):
            mu = jnp.mean(x, axis=-1, keepdims=True)
            var = jnp.var(x, axis=-1, keepdims=True)
            return (x - mu) / jnp.sqrt(var + LN_EPS) * g + b

        def balanced_assignment(scores):
            T, E = scores.shape
            C = T // E
            taken = jnp.zeros((T,), dtype=bool)
            parts = []
            for e in range(E):
                s = jnp.where(taken, -jnp.inf, scores[:, e])
                _, idx = jax.lax.top_k(s, C)
                parts.append(idx)
                taken = taken.at[idx].set(True)
            return jnp.concatenate(parts)
        D = x.shape[-1]
        feat = x.reshape(-1, D)
        T = feat.shape[0]
        E = centroids.shape[0]
        C = T // E
        norm = layer_norm(feat, ln_g, ln_b)
        scores = jax.lax.stop_gradient(norm @ centroids.T)
        sort_by_expert = balanced_assignment(scores)
        routed = feat[sort_by_expert].reshape(E, C, D)
        h = layer_norm(routed, ln_g, ln_b)
        h = jax.nn.gelu(jnp.einsum('ecd,edf->ecf', h, w1) + b1[:, None, :])
        h = jnp.einsum('ecf,efd->ecd', h, w2) + b2[:, None, :]
        out = routed + h
        inv = jnp.zeros((T,), dtype=jnp.int32).at[sort_by_expert].set(jnp.arange(T, dtype=jnp.int32))
        return out.reshape(T, D)[inv].reshape(x.shape)
    x = L0_attn_x
    xn = _layernorm(x, axis=-1)
    x = x + _L0_attn_ref(xn, L0_attn_Wq, L0_attn_Wk, L0_attn_Wv, L0_attn_Wo, L0_attn_qn_w, L0_attn_kn_w) + _L0_ffn_ref(xn, L0_ffn_centroids, L0_ffn_ln_g, L0_ffn_ln_b, L0_ffn_w1, L0_ffn_b1, L0_ffn_w2, L0_ffn_b2)
    return x

_drawn_inputs = setup_inputs


def setup_inputs(seed=0):
    import zlib

    import numpy as np

    out = dict(_drawn_inputs(seed))
    spreads = {'L0_attn_qn_w': (1.0, 0.6),
     'L0_attn_kn_w': (1.0, 0.6),
     'L0_ffn_ln_g': (1.0, 0.2),
     'L0_ffn_ln_b': (0.0, 0.8),
     'L0_ffn_b1': (0.0, 0.43),
     'L0_ffn_b2': (0.0, 0.1)}
    factors = {'L0_attn_Wq': 8.0, 'L0_attn_Wk': 8.0, 'L0_attn_Wv': 8.0, 'L0_attn_Wo': 8.0}
    for name, (base, spread) in spreads.items():
        noise = np.random.default_rng([zlib.crc32(name.encode()), seed]).standard_normal(out[name].shape)
        drawn = base * np.exp(spread * noise) if base else spread * noise
        out[name] = jnp.asarray(drawn.astype(out[name].dtype))
    for name, factor in factors.items():
        out[name] = (out[name] * factor).astype(out[name].dtype)
    return out
```

```python
import numpy as np
import concourse.bass as bass
from concourse import mybir
from contextlib import ExitStack

F32 = mybir.dt.float32
F32R = mybir.dt.float32r
BF16 = mybir.dt.bfloat16
I32 = mybir.dt.int32
U32 = mybir.dt.uint32
ALU = mybir.AluOpType
ACT = mybir.ActivationFunctionType
AX = mybir.AxisListType

B, N, D = 16, 512, 256
H, DH = 16, 16
E, F = 8, 1024
T = B * N
C = T // E
P = 128
NT = T // P
CH = N // P
KD = D // P
HU = P // DH
NFC = F // P
LN_EPS = 1e-5
RMS_EPS = float(np.finfo(np.float32).eps)
SCALE = DH ** -0.5
ROW_SHIFT, ROWS = 64, 96
SAFE_BOUND = 60.0
BITS = 3
STEPS = -(-32 // BITS)
CAND = 2 ** BITS - 1


class Phase:

    def __init__(self, nc, name, ctx, last_stage):
        self.nc, self.name, self.ctx, self.last = nc, name, ctx, last_stage
        self.queue, self.where, self.sems, self.per = {}, {}, {}, {}
        self.first = {}
        self.apart = set()

    def sem(self, name):
        if name not in self.sems:
            self.sems[name] = self.ctx.enter_context(self.nc.semaphore(f"{self.name}_{name}"))
            self.per[name] = 0
        return name

    def op(self, eng, fn, after=(), key=None, stage=1, group=""):
        if key is not None:
            s = self.sem(f"{eng}{group}")
            self.per[s] += 1
            assert key not in self.where, key
            self.where[key] = (s, self.per[s])
        self.queue.setdefault(eng, []).append((fn, tuple(after), key, stage, group, 1))

    def dma(self, eng, fns, after=(), key=None, stage=1, group=""):
        s = self.sem("dma_" + "_".join(map(str, key)) if isinstance(key, tuple) else f"dma_{key}")
        self.per[s] += 16 * len(fns)
        self.where[key] = (s, self.per[s])
        if eng == "gpsimd":
            self.first[s] = stage - 1

        def issue(e, it):
            for f in fns:
                f(e, it).then_inc(self.sems[s], 16)
            return None
        self.queue.setdefault(eng, []).append((issue, tuple(after), key, stage, group, 16 * len(fns)))

    def value(self, step, it):
        s, k = self.where[step]
        return self.sems[s], (it - self.first.get(s, -1)) * self.per[s] + k

    def wait(self, e, after, it, apart):
        for a in after:
            back = 0
            if a[0] == "prev":
                back, a = 1, a[1]
            if back and isinstance(it, int) and self.value(a, it - back)[1] <= 0:
                continue
            e.wait_ge(*self.value(a, it - back))
            if apart and not isinstance(it, int):
                e.nop(nofuse=True)

    def body(self, eng, e, it, stages, groups):
        skipped = {}
        waited = {}

        def settle():
            for s, n in skipped.items():
                e.drain()
                e.sem_inc(self.sems[s], n)
            skipped.clear()

        for fn, after, key, stage, group, n in self.queue.get(eng, []):
            if stage not in stages or group not in groups:
                name = self.where[key][0] if key else ""
                over = not key or name in self.first or (name.startswith("dma_") and stage < min(stages))
                if not over and group in groups:
                    s = self.where[key][0]
                    skipped[s] = skipped.get(s, 0) + n
                continue
            settle()
            need = []
            for a in after:
                back, b = (1, a[1]) if a[0] == "prev" else (0, a)
                if b not in self.where:
                    raise KeyError(b)
                s, k = self.where[b]
                if waited.get(s, (-9, 0)) < (-back, k):
                    waited[s] = (-back, k)
                    need.append(a)
            self.wait(e, need, it, eng in ("gpsimd", "sync") or key in self.apart)
            ins = fn(e, it)
            if key is not None and ins is not None:
                ins.then_inc(self.sems[self.where[key][0]], 1)
        settle()


def on_engine(block, eng):
    return {"sync": block.sync, "scalar": block.scalar, "vector": block.vector,
            "gpsimd": block.gpsimd, "tensor": block.tensor}[eng]


def run_phase(nc, phase, engines, plan):
    with nc.Block() as block:
        for eng in engines:
            def program(e, eng=eng):
                for its, stages, groups in plan:
                    if isinstance(its, int):
                        phase.body(eng, e, its, stages, groups)
                    elif any(x[3] in stages and x[4] in groups for x in phase.queue.get(eng, [])):
                        with e.Fori(its[0], its[1]) as it:
                            phase.body(eng, e, it, stages, groups)
            on_engine(block, eng)(program)


def build(nc, a, out):
    x_rows = a["x"].rearrange("b n d -> (b n) d")
    x_batch = a["x"].rearrange("b (c p) d -> b p c d", p=P)
    attn_dram = nc.dram_tensor("attn_rows", (T, D), F32, kind="Internal").ap()
    order_dram = nc.dram_tensor("order", (T, 1), I32, kind="Internal").ap()
    parts_dram = nc.dram_tensor("parts", (2, 2, 2, P, N), F32, kind="Internal").ap()
    shift_dram = nc.dram_tensor("shifts", (2, HU * CH, P), F32, kind="Internal").ap()

    with ExitStack() as top:
        def sb(name, shape, dt, ctx=top):
            return ctx.enter_context(nc.sbuf_tensor(name, shape, dt))

        k = {}
        k["ident"] = sb("ident", [P, P], F32)
        k["gain"] = sb("gain", [P, KD], F32)
        k["offset"] = sb("offset", [P, KD], F32)
        k["eps_ln"] = sb("eps_ln", [P, CH], F32)
        k["half"] = sb("half", [P, CH], F32)
        k["mean"] = sb("mean", [P, NT], F32)
        k["rstd"] = sb("rstd", [P, NT], F32)
        k["tokens"] = sb("tokens", [P, NT], I32)
        k["slot_i"] = sb("slot_i", [P, NT], I32)
        with ExitStack() as mid:
            k["scores"] = sb("scores", [P, E, NT], F32, mid)
            statistics_and_scores(nc, a, x_batch, k)
            attention_and_routing(nc, a, x_batch, attn_dram, order_dram, parts_dram, shift_dram, k)
        experts(nc, a, x_rows, attn_dram, order_dram, out, k)


class LayerNorm:

    def __init__(self, ph, tag, src, tiles, k, dst, stage):
        self.ph, self.tag, self.src, self.k, self.dst, self.stage = ph, tag, src, k, dst, stage
        self.stats, self.aggr, self.veps, self.rstd = tiles

    def moments(self, after, free_aggr=()):
        ph, tag, stage, k = self.ph, self.tag, self.stage, self.k

        def stat(e, it):
            for c in range(CH):
                ins = e.bn_stats(self.stats[:, c, :], self.src[:, c, :])
            return ins
        ph.op("vector", stat, after, (tag, "stat"), stage)

        def agg(e, it):
            for c in range(CH):
                ins = e.bn_aggr(self.aggr[:, c, :], self.stats[:, c, :])
            return ins
        ph.apart.add((tag, "agg"))
        ph.op("vector", agg, [(tag, "stat"), *free_aggr], (tag, "agg"), stage)
        ph.op("gpsimd", lambda e, it: e.tensor_tensor(self.veps[:, :], self.aggr[:, :, 1], k["eps_ln"][:, :], ALU.add),
              [(tag, "agg")], (tag, "veps"), stage)
        ph.op("gpsimd", lambda e, it: e.tensor_tensor(self.rstd[:, :], self.veps[:, :], k["half"][:, :], ALU.pow),
              [(tag, "veps")], (tag, "rstd"), stage)

    def scale(self, free_dst=()):
        def fn(e, it):
            for c in range(CH):
                ins = e.tensor_scalar(self.dst[:, c, :], self.src[:, c, :], self.aggr[:, c, 0:1],
                                      self.rstd[:, c:c + 1], ALU.subtract, ALU.mult)
            return ins
        self.ph.op("vector", fn, [(self.tag, "rstd"), *free_dst], (self.tag, "out"), self.stage)


def statistics_and_scores(nc, a, x_batch, k):
    with ExitStack() as ctx:
        def sb(name, shape, dt):
            return ctx.enter_context(nc.sbuf_tensor(name, shape, dt))

        cent = sb("cent", [P, KD, E], F32)
        xb = [sb(f"s_x{r}", [P, CH, D], F32) for r in range(2)]
        xn = [sb(f"s_xn{r}", [P, CH, D], F32) for r in range(2)]
        z = [sb(f"s_z{r}", [P, CH, D], F32) for r in range(2)]
        normT = [sb(f"s_nT{r}", [P, KD, N], F32) for r in range(2)]
        small = [[sb(f"s_{n}{r}{i}", s, F32) for n, s in
                  (("st", [P, CH, 6]), ("mv", [P, CH, 2]), ("ve", [P, CH]), ("rs", [P, CH]))]
                 for r in range(2) for i in range(2)]
        turned = [[ctx.enter_context(nc.psum_tensor(f"s_t{r}{d}", [P, N], F32)) for d in range(KD)]
                  for r in range(2)]
        score = [ctx.enter_context(nc.psum_tensor(f"s_s{r}", [P, CH, E], F32)) for r in range(2)]
        s_const, s_pool = (ctx.enter_context(nc.semaphore(n)) for n in ("s_const", "s_pool"))

        with nc.Block() as block:
            @block.sync
            def _(e):
                loads = [(k["ident"][:, :], a["ident"]), (k["gain"][:, :], a["ln_g"]),
                         (k["offset"][:, :], a["ln_b"]), (k["tokens"][:, :], a["tokens"]),
                         (cent[:, :, :], a["centroids"])]
                for dst, src in loads:
                    e.dma_start(dst, src).then_inc(s_const, 16)
                e.wait_ge(s_const, 16 * len(loads))

            @block.gpsimd
            def _(e):
                e.memset(k["eps_ln"][:, :], LN_EPS)
                e.memset(k["half"][:, :], -0.5).then_inc(s_pool, 1)
                e.wait_ge(s_pool, 1)

        ph = Phase(nc, "s", ctx, 2)
        R2 = range(2)

        def first(it, r, stage):
            return CH * (2 * (it + 1 - stage) + r)

        norm = [[LayerNorm(ph, f"a{r}", xb[r], small[2 * r], k, xn[r], 0),
                 LayerNorm(ph, f"b{r}", xn[r], small[2 * r + 1], k, z[r], 1)] for r in R2]
        for r in R2:
            ph.dma("sync", [lambda e, it, r=r: e.dma_start(xb[r][:, :, :], x_batch[2 * (it + 1) + r])],
                   [("prev", (f"a{r}", "out"))], ("x", r), 0)
        for r in R2:
            for d in range(KD):
                def turn(e, it, r=r, d=d):
                    for c in range(CH):
                        ins = e.transpose(turned[r][d][:, c * P:(c + 1) * P],
                                          z[r][:, c, d * P:(d + 1) * P], k["ident"][:, :])
                    return ins
                ph.op("tensor", turn, [("prev", (f"b{r}", "out")), ("prev", ("gain", r, d))], ("turn", r, d), 2)
                ph.op("scalar", lambda e, it, r=r, d=d: e.activation(
                    normT[r][:, d, :], turned[r][d][:, :], ACT.Identity, bias=k["offset"][:, d:d + 1],
                    scale=k["gain"][:, d:d + 1]), [("turn", r, d), ("prev", ("score", r))], ("gain", r, d), 2)
        for r in R2:
            def score_mm(e, it, r=r):
                for c in range(CH):
                    for d in range(KD):
                        ins = e.matmul(score[r][:, c, :], normT[r][:, d, c * P:(c + 1) * P],
                                       cent[:, d, :], start=(d == 0), stop=(d == KD - 1))
                return ins
            ph.op("tensor", score_mm, [("gain", r, KD - 1), ("prev", ("keep", r))], ("score", r), 2)
        for r in R2:
            norm[r][1].moments([("prev", (f"a{r}", "out"))])
        for r in R2:
            norm[r][0].moments([("x", r)], [("prev", (f"kept{r}",))])
        for r in R2:
            norm[r][1].scale([("turn", r, KD - 1)])
        for r in R2:
            norm[r][0].scale([(f"b{r}", "out")])

            def keep(e, it, r=r):
                at = bass.ds(first(it, r, 0), CH)
                e.tensor_copy(k["rstd"][:, at], norm[r][0].rstd[:, :])
                return e.tensor_copy(k["mean"][:, at], norm[r][0].aggr[:, :, 0])
            ph.op("gpsimd", keep, [(f"a{r}", "rstd")], (f"kept{r}",), 0)
        for r in R2:
            ph.op("vector", lambda e, it, r=r: e.tensor_copy(
                k["scores"][:, :, bass.ds(first(it, r, 2), CH)].rearrange("p e c -> p c e"), score[r][:, :, :]),
                [("score", r)], ("keep", r), 2)
        n = B // 2
        run_phase(nc, ph, ["sync", "vector", "gpsimd", "tensor", "scalar"],
                  [(-1, {0}, {""}), (0, {0, 1}, {""}), ((1, n - 1), {0, 1, 2}, {""}), (n - 1, {1, 2}, {""}), (n, {2}, {""})])


def split_weights(nc, ctx, block, jobs, raw, sem_load, sem_hi, sem_lo):
    @block.sync
    def _(e):
        for (src, _, _), land in zip(jobs, raw):
            e.dma_start(land[:, :, :], src).then_inc(sem_load, 16)
        e.wait_ge(sem_load, 16 * len(jobs))

    @block.scalar
    def _(e):
        e.preload_act_table_set("natural_log_exp_and_others")
        e.wait_ge(sem_load, 16 * len(jobs))
        for (_, hi, _), land in zip(jobs, raw):
            e.activation(hi[:, :, :], land[:, :, :], ACT.Copy).then_inc(sem_hi, 1)

    @block.vector
    def _(e):
        for i, ((_, hi, lo), land) in enumerate(zip(jobs, raw)):
            e.wait_ge(sem_hi, i + 1)
            e.tensor_tensor(lo[:, :, :], land[:, :, :], hi[:, :, :].bitcast(F32), ALU.subtract).then_inc(sem_lo, 1)


def attention_and_routing(nc, a, x_batch, attn_dram, order_dram, parts_dram, shift_dram, k):
    G = 4
    VW = 32
    with ExitStack() as ctx:
        def sb(name, shape, dt):
            return ctx.enter_context(nc.sbuf_tensor(name, shape, dt))

        def ps(name, shape):
            return ctx.enter_context(nc.psum_tensor(name, shape, F32))

        ctx.enter_context(nc.allow_low_precision(reason="counts of at most NT tokens are exact in bfloat16"))
        w = {n: [sb(f"w{n}{i}", [P, KD, D], F32R) for i in range(2)] for n in "qkv"}
        wo = sb("wo", [P, KD, D], F32)
        headsum = sb("headsum", [P, P], F32)
        ones_h = sb("ones_h", [P, P], BF16)
        below = sb("below", [P, P], BF16)
        qk_w = sb("qk_w", [P, 2], F32)
        wq_scale = sb("wq_scale", [P, 1], F32)
        eps_rms = sb("eps_rms", [P, 1], F32)
        flag_f = sb("flag_f", [1, 2], F32)
        flag = sb("flag", [1, 1], I32)
        xb = sb("xb", [P, CH, D], F32)
        xn = sb("xn", [P, CH, D], F32)
        xT = [sb(f"xT{i}", [P, KD, N], F32R) for i in range(2)]
        raw = {n: sb(f"raw{n}", [P, N], F32) for n in "qk"}
        sq = {n: sb(f"sq{n}", [P, N], F32) for n in "qk"}
        inv = {n: sb(f"inv{n}", [P, N], F32) for n in "qk"}
        full = {n: sb(f"full{n}", [P, N], F32) for n in "qk"}
        part = {n: [sb(f"part{n}{i}", [P, N], F32R) for i in range(2)] for n in "qk"}
        stack = {n: [sb(f"stack{n}{u}", [ROWS, HU, N], F32R) for u in range(2)] for n in "qk"}
        v = [sb(f"v{u}", [P, CH, HU, VW], F32) for u in range(2)]
        prob = [sb(f"prob{i}", [P, G, 2, N], F32) for i in range(2)]
        oT = [sb(f"oT{i}", [P, N], F32) for i in range(2)]
        rden = [sb(f"rden{i}", [P, CH, G], F32) for i in range(2)]
        o_tok = sb("o_tok", [P, CH, D], F32)
        oT2 = sb("oT2", [P, KD, N], F32)
        ao = sb("ao", [P, CH, D], F32)
        mx = sb("mx", [P, HU * CH], F32)
        sh = [sb(f"sh{i}", [HU * CH, P], F32R) for i in range(2)]
        shf = sb("shf", [HU * CH, P], F32)
        cand_bits = sb("cand_bits", [P, STEPS, CAND], I32)
        steps_f = sb("steps_f", [P, STEPS], F32)
        zc = sb("zc", [P, CAND], I32)
        sgn = sb("sgn", [P, CAND], I32)
        thr = sb("thr", [P, CAND], I32)
        zcur = sb("zcur", [P, 1], I32)
        zadd = sb("zadd", [P, 1], U32)
        digit = sb("digit", [P, 1], F32)
        ge = sb("ge", [P, CAND, NT], F32)
        part_cnt = sb("part_cnt", [P, CAND], BF16)
        gem = sb("gem", [P, CAND], F32)
        gt = sb("gt", [P, NT], BF16)
        gt_cnt = sb("gt_cnt", [P, 1], BF16)
        eq = sb("eq", [P, NT], BF16)
        need = sb("need", [P, 1], F32)
        cols = sb("cols", [P, NT], F32)
        zero = sb("zero", [P, NT], F32)
        csum = sb("csum", [P, NT], F32)
        rank = sb("rank", [P, NT], F32)
        tie = sb("tie", [P, NT], F32)
        sel = sb("sel", [P, NT], BF16)
        sel_i = sb("sel_i", [P, NT], I32)
        rank2 = sb("rank2", [P, NT], F32)
        slot = sb("slot", [P, NT], F32)
        base = sb("base", [P, 1], F32)
        lowest = sb("lowest", [P, 1], F32)

        S = [ps(f"S{i}", [P, 2, N]) for i in range(2)]
        pv = ps("pv", [P, N])
        W = [ps(f"W{i}", [P, N]) for i in range(2)]
        R = ps("R", [P, N])

        sems = [ctx.enter_context(nc.semaphore(n)) for n in ("a_ld", "a_hi", "a_lo", "a_c", "a_v", "a_t", "a_p", "a_f")]
        s_ld, s_hi, s_lo, s_c, s_v, s_t, s_p, s_f = sems
        with nc.Block() as block:
            jobs = [(a[f"w{n}"], w[n][0], w[n][1]) for n in "qkv"]
            split_weights(nc, ctx, block, jobs, [t[:, 0:KD, :] for t in (xb, xn, o_tok)], s_ld, s_hi, s_lo)
        with nc.Block() as block:
            @block.sync
            def _(e):
                loads = [(wo[:, :, :], a["wo"]), (headsum[:, :], a["headsum"]), (qk_w[:, :], a["qk_w"]),
                         (cand_bits[:, :, :], a["cand_bits"]), (steps_f[:, :], a["steps_f"])]
                for dst, src in loads:
                    e.dma_start(dst, src).then_inc(s_c, 16)
                e.wait_ge(s_c, 16 * len(loads))

            @block.vector
            def _(e):
                done = 0
                for t, val in ((eps_rms, RMS_EPS), (lowest, float(np.finfo(np.float32).min)), (base, 0.0), (slot, 0.0), (zero, 0.0), (ones_h, 1.0)):
                    e.memset(t[:, :], val)
                for u in range(2):
                    e.memset(v[u][:, :, :, :], 1.0)
                    for n in "qk":
                        e.memset(stack[n][u][:, :, :].bitcast(F32), 0.0).then_inc(s_v, 1)
                        done += 1
                e.wait_ge(s_v, done)
                for u in range(2):
                    e.memset(stack["k"][u][ROW_SHIFT:ROW_SHIFT + 2, :, :].bitcast(F32), 1.0)
                e.wait_ge(s_c, 16 * 5)
                e.scalar_tensor_tensor(wq_scale[:, :], qk_w[:, 0:1], SCALE, qk_w[:, 1:2], ALU.mult, ALU.mult).then_inc(s_v, 1)
                e.wait_ge(s_t, 1)
                e.tensor_reduce(flag_f[:, 0:1], R[0:1, 0:P], AX.X, ALU.max, apply_absolute_value=True).then_inc(s_v, 1)
                e.wait_ge(s_v, done + 2)
                e.tensor_scalar(flag[:, :], flag_f[:, 0:1], SAFE_BOUND / DH, None, ALU.is_gt).then_inc(s_v, 1)

            @block.gpsimd
            def _(e):
                e.memset(below[:, :], 1.0).then_inc(s_p, 1)
                e.wait_ge(s_p, 1)
                e.affine_select(out=below[:, :], in_=below[:, :], compare_op=ALU.is_ge, fill=0.0,
                                base=-1, pattern=[[1, P]], channel_multiplier=-1).then_inc(s_p, 1)

            @block.tensor
            def _(e):
                e.wait_ge(s_v, 5)
                e.transpose(R[0:1, 0:P], wq_scale[:, :], k["ident"][:, :]).then_inc(s_t, 1)

        ph = Phase(nc, "a", ctx, 2)
        job_release = []

        def job(fill, after, key, release, stage=1):
            j = len(job_release)
            free = ("prev", job_release_tail[j % 2]) if j < 2 else job_release[j - 2]
            job_release.append(release)
            bank = W[j % 2]
            ph.op("tensor", lambda e, it: fill(e, it, bank), [*after, free], key, stage)
            return bank

        job_release_tail = [("v", 0), ("onorm", 2)]

        def batch(it, stage):
            return it + 1 - stage

        def load_x():
            ph.dma("sync", [lambda e, it: e.dma_start(xb[:, :, :], x_batch[batch(it, 0)])],
                   [("prev", ("xn",))], ("x",), 0)

        def norm_x():
            def fn(e, it):
                b = batch(it, 0)
                for c in range(CH):
                    ins = e.tensor_scalar(xn[:, c, :], xb[:, c, :], k["mean"][:, bass.ds(CH * b + c, 1)],
                                          k["rstd"][:, bass.ds(CH * b + c, 1)], ALU.subtract, ALU.mult)
                return ins
            ph.op("vector", fn, [("x",), ("prev", ("xturn", KD - 1))], ("xn",), 0)

        def turn_x(d):
            def fn(e, it, bank):
                for c in range(CH):
                    ins = e.transpose(bank[:, c * P:(c + 1) * P], xn[:, c, d * P:(d + 1) * P], k["ident"][:, :])
                return ins
            bank = job(fn, [("xn",)], ("xturn", d), ("xlo", d), 0)
            ph.op("scalar", lambda e, it: e.activation(xT[0][:, d, :], bank[:, :], ACT.Copy),
                  [("xturn", d), ("vproj", 1)], ("xhi", d), 0)
            ph.op("vector", lambda e, it: e.tensor_tensor(xT[1][:, d, :], bank[:, :], xT[0][:, d, :].bitcast(F32), ALU.subtract),
                  [("xhi", d)], ("xlo", d), 0)

        PRODUCTS = ((0, 0), (0, 1), (1, 0))

        def ready_x(u):
            return [("prev", ("xlo", KD - 1)) if u else ("xlo", KD - 1)]

        def project(n, u, stage):
            def fn(e, it, bank):
                for i, (d, (pw, px)) in enumerate((d, pr) for d in range(KD) for pr in PRODUCTS):
                    ins = e.matmul(bank[:, :], w[n][pw][:, d, u * P:(u + 1) * P], xT[px][:, d, :],
                                   start=(i == 0), stop=(i == KD * len(PRODUCTS) - 1))
                return ins
            bank = job(fn, ready_x(u), (n, "proj", u), (n, "raw", u), stage)
            ph.op("vector", lambda e, it: e.tensor_copy(raw[n][:, :], bank[:, :]), [(n, "proj", u)], (n, "raw", u), stage)
            ph.op("gpsimd", lambda e, it: e.tensor_tensor(sq[n][:, :], raw[n][:, :], raw[n][:, :], ALU.mult),
                  [(n, "raw", u)], (n, "sq", u), stage)

        def rms(n, u, stage):
            bank = job(lambda e, it, bank: e.matmul(bank[:, :], headsum[:, :], sq[n][:, :], start=True, stop=True),
                       [(n, "sq", u)], (n, "ms", u), (n, "ln", u), stage)
            ph.op("scalar", lambda e, it: e.activation(inv[n][:, :], bank[:, :], ACT.Ln, bias=eps_rms[:, 0:1], scale=1.0 / DH),
                  [(n, "ms", u)], (n, "ln", u), stage)
            ph.op("scalar", lambda e, it: e.activation(inv[n][:, :], inv[n][:, :], ACT.Exp, scale=-0.5),
                  [(n, "ln", u)], (n, "inv", u), stage)

        def parts(n, u, stage):
            weight = wq_scale[:, 0:1] if n == "q" else 1.0
            ph.op("vector", lambda e, it: e.scalar_tensor_tensor(full[n][:, :], raw[n][:, :], weight, inv[n][:, :], ALU.mult, ALU.mult),
                  [(n, "inv", u), ("prev", (n, "lo", 0)) if u else (n, "lo", 1)], (n, "full", u), stage)
            out_before = ("prev", (n, "out", 0)) if u else (n, "out", 1)
            ph.op("vector", lambda e, it: e.tensor_copy(part[n][0][:, :], full[n][:, :]),
                  [(n, "full", u), out_before], (n, "hi", u), stage)
            ph.op("gpsimd", lambda e, it: e.tensor_tensor(part[n][1][:, :], full[n][:, :], part[n][0][:, :].bitcast(F32), ALU.subtract),
                  [(n, "hi", u)], (n, "lo", u), stage)
            i = "qk".index(n)
            ph.dma("sync", [lambda e, it, p=p: e.dma_start(parts_dram[u, i, p], part[n][p][:, :].bitcast(F32)) for p in range(2)],
                   [(n, "lo", u), ("prev", (n, "stack", u))], (n, "out", u), stage)
            order = (0, 0, 1) if n == "q" else (0, 1, 0)
            src = parts_dram[u, i].rearrange("s (h d) n -> s d h n", d=DH)
            last = ("qk_done", u)
            free = ("prev", last) if u == 1 or stage else last
            ph.dma("sync", [lambda e, it, r=r, p=p: e.dma_start(stack[n][u][r * DH:(r + 1) * DH, :, :].bitcast(F32), src[p])
                            for r, p in enumerate(order)],
                   [(n, "out", u), free], (n, "stack", u), stage)

        def project_v(u, stage):
            def fn(e, it, bank):
                for c in range(CH):
                    for i, (d, (px, pw)) in enumerate((d, pr) for d in range(KD) for pr in PRODUCTS):
                        ins = e.matmul(bank[:, c * P:(c + 1) * P], xT[px][:, d, c * P:(c + 1) * P],
                                       w["v"][pw][:, d, u * P:(u + 1) * P],
                                       start=(i == 0), stop=(i == KD * len(PRODUCTS) - 1))
                return ins
            bank = job(fn, ready_x(u), ("vproj", u), ("v", u), stage)
            busy = ("prev", ("pv_done", u)) if u == 1 else ("pv_done", u)
            ph.op("vector", lambda e, it: e.tensor_copy(
                v[u][:, :, :, 0:DH], bank[:, :].rearrange("p (c h d) -> p c h d", c=CH, h=HU)),
                [("vproj", u), busy], ("v", u), stage)

        s_g = {n: ctx.enter_context(nc.semaphore(f"g_{n}")) for n in ("mm", "red", "neg", "tp", "sh", "dma")}
        needed = {}

        def shift(u):
            pairs = HU * CH // 2

            def n_of(it):
                return 2 * it + u

            def pe(e, it):
                for i in range(pairs):
                    h, c0 = i // 2, 2 * (i % 2)
                    if i >= 2:
                        e.wait_ge(s_g["red"], pairs * n_of(it) + i - 1)
                    for c in range(2):
                        ins = e.matmul(S[i % 2][:, c, :], stack["q"][u][0:3 * DH, h, (c0 + c) * P:(c0 + c + 1) * P],
                                       stack["k"][u][0:3 * DH, h, :], start=True, stop=True)
                    ins.then_inc(s_g["mm"], 1)
                e.wait_ge(s_g["neg"], n_of(it) + 1)
                e.transpose(S[0][0:HU * CH, 0, 0:P], mx[:, :], k["ident"][:, :]).then_inc(s_g["tp"], 1)
                e.wait_ge(s_g["sh"], 3 * n_of(it) + 3)
                e.wait_ge(s_g["dma"], 64 * n_of(it) + 64)

            def dve(e, it):
                for i in range(pairs):
                    e.wait_ge(s_g["mm"], pairs * n_of(it) + i + 1)
                    e.tensor_reduce(mx[:, 2 * i:2 * i + 2], S[i % 2][:, :, :], AX.X, ALU.max).then_inc(s_g["red"], 1)
                e.wait_ge(s_g["red"], pairs * n_of(it) + pairs)
                e.tensor_scalar(mx[:, :], mx[:, :], -1.0, None, ALU.mult).then_inc(s_g["neg"], 1)
                e.wait_ge(s_g["tp"], n_of(it) + 1)
                e.tensor_copy(shf[:, :], S[0][0:HU * CH, 0, 0:P]).then_inc(s_g["sh"], 1)
                e.wait_ge(s_g["sh"], 3 * n_of(it) + 1)
                e.tensor_copy(sh[0][:, :], shf[:, :]).then_inc(s_g["sh"], 1)
                e.wait_ge(s_g["sh"], 3 * n_of(it) + 2)
                e.tensor_tensor(sh[1][:, :], shf[:, :], sh[0][:, :].bitcast(F32), ALU.subtract).then_inc(s_g["sh"], 1)

            def sp(e, it):
                e.wait_ge(s_g["sh"], 3 * n_of(it) + 3)
                e.nop(nofuse=True)
                for i in range(2):
                    e.dma_start(shift_dram[i], sh[i][:, :].bitcast(F32)).then_inc(s_g["dma"], 16)
                e.wait_ge(s_g["dma"], 64 * n_of(it) + 32)
                e.nop(nofuse=True)
                for i in range(2):
                    r = ROW_SHIFT + i
                    e.dma_start(stack["q"][u][r:r + 1, :, :].bitcast(F32),
                                shift_dram[i].rearrange("(o h c) q -> o h (c q)", o=1, h=HU)).then_inc(s_g["dma"], 16)
                e.wait_ge(s_g["dma"], 64 * n_of(it) + 64)
                e.nop(nofuse=True)

            def only(eng, fn):
                def run(e, it):
                    with e.If(needed[eng] > 0):
                        fn(e, it)
                    return None
                return run
            before = [("q", "stack", u), ("k", "stack", u)]
            if u == 0:
                before = [("prev", x) for x in before]
            exp_before = ("exp", 3, G - 1) if u else ("prev", ("exp", 7, G - 1))
            ph.op("tensor", only("tensor", pe), [*before, exp_before])
            ph.op("vector", only("vector", dve))
            ph.op("sync", only("sync", sp))

        def heads(s, j):
            u, g, half = s // 4, s % 4 // 2, s % 2
            h = G * g + j
            st = [("q", "stack", u), ("k", "stack", u)]
            if u == 0:
                st = [("prev", x) for x in st]
            n = G * s + j
            free = [("exp", (n - 2) // G, (n - 2) % G)] if n >= 2 else [("prev", ("exp", 7, G - 2 + n))]

            def fn(e, it):
                for c in range(2):
                    key = 2 * half + c
                    ins = e.matmul(S[j % 2][:, c, :], stack["k"][u][:, h, key * P:(key + 1) * P],
                                   stack["q"][u][:, h, :], start=True, stop=True)
                return ins
            key = ("qk_done", u) if (s % 4 == 3 and j == G - 1) else ("qk", s, j)
            ph.op("tensor", fn, [*st, *free], key)
            freed = [("pv", s - 2, 1)] if s >= 2 else [("prev", ("pv", 6 + s, 1) if s == 0 else ("pv_done", 1))]
            freed = [x if x != ("pv", 3, 1) else ("pv_done", 0) for x in freed]
            ph.op("scalar", lambda e, it: e.activation(prob[s % 2][:, j, :, :], S[j % 2][:, :, :], ACT.Exp),
                  [key, *freed], ("exp", s, j))

        def weigh(s, c):
            u, g, half = s // 4, s % 4 // 2, s % 2

            def fn(e, it):
                for j in range(G):
                    ins = e.matmul(pv[VW * j:VW * (j + 1), :], v[u][:, 2 * half + c, G * g + j, :],
                                   prob[s % 2][:, j, c, :], start=(half == 0 and c == 0), stop=(half == 1 and c == 1))
                return ins
            after = [("exp", s, G - 1), ("v", u) if u else ("prev", ("v", u))]
            q = s // 2
            if half == 0 and c == 0:
                after.append(("pvcopy", q - 1) if q else ("prev", ("pvcopy", 3)))
            key = ("pv_done", u) if (s % 4 == 3 and c == 1) else ("pv", s, c)
            ph.op("tensor", fn, after, key)
            if half == 1 and c == 1:
                turned_before = ("prev", ("oturn", q + 2)) if q < 2 else ("oturn", q - 2)
                if q == 1:
                    turned_before = ("oturn", 3)
                ph.op("vector", lambda e, it: e.tensor_copy(oT[q % 2][:, :], pv[:, :]), [key, turned_before], ("pvcopy", q))

        def normalise(q, stage=1):
            def fn(e, it, bank):
                for c in range(CH):
                    ins = e.transpose(bank[:, c * P:(c + 1) * P], oT[q % 2][:, c * P:(c + 1) * P], k["ident"][:, :])
                return ins
            bank = job(fn, [("pvcopy", q) if stage == 1 else ("prev", ("pvcopy", q))], ("oturn", q), ("onorm", q), stage)
            seen = bank[:, :].rearrange("p (c j w) -> p c j w", c=CH, j=G)
            r = rden[q % 2]
            ph.op("vector", lambda e, it: e.reciprocal(r[:, :, :], seen[:, :, :, DH]), [("oturn", q)], ("rden", q), stage)
            free = [("o2turn", KD - 1)] if q == 0 else []
            ph.op("vector", lambda e, it: e.tensor_tensor(
                o_tok[:, :, G * DH * q:G * DH * (q + 1)].rearrange("p c (j d) -> p c j d", j=G),
                seen[:, :, :, 0:DH], r[:, :, :].unsqueeze(3).broadcast_to([P, CH, G, DH]), ALU.mult),
                [("rden", q), *free], ("onorm", q), stage)

        def turn_o(d):
            def fn(e, it, bank):
                for c in range(CH):
                    ins = e.transpose(bank[:, c * P:(c + 1) * P], o_tok[:, c, d * P:(d + 1) * P], k["ident"][:, :])
                return ins
            bank = job(fn, [("onorm", 3)], ("o2turn", d), ("o2", d), 2)
            ph.op("scalar", lambda e, it: e.activation(oT2[:, d, :], bank[:, :], ACT.Copy),
                  [("o2turn", d), ("prev", ("wo", 1))], ("o2", d), 2)

        def project_o(i):
            def fn(e, it, bank):
                for c in range(2):
                    for d in range(KD):
                        ins = e.matmul(bank[:, c * D:(c + 1) * D], oT2[:, d, (2 * i + c) * P:(2 * i + c + 1) * P],
                                       wo[:, d, :], start=(d == 0), stop=(d == KD - 1))
                return ins
            bank = job(fn, [("o2", KD - 1)], ("wo", i), ("woe", i), 2)
            ph.op("vector", lambda e, it: e.tensor_copy(ao[:, 2 * i:2 * i + 2, :], bank[:, :].rearrange("p (c d) -> p c d", c=2)),
                  [("wo", i), ("prev", ("attn",))], ("woe", i), 2)
            if i == 1:
                ph.dma("sync", [lambda e, it: e.dma_start(
                    attn_dram.rearrange("(b c p) d -> b p c d", c=CH, p=P)[it - 1], ao[:, :, :])],
                    [("woe", 0), ("woe", 1)], ("attn",), 2)

        def route(fn, eng="vector", after=(), key=None):
            ph.op(eng, fn, after, key, 1, "route")

        def bits_ask(i):
            before = ("r_z", i - 1) if i else ("r_init",)
            if i == 0:
                route(lambda e, it: e.memset(zcur[:, :], -2 ** 31), after=[("prev", ("r_taken",))], key=("r_init",))
            route(lambda e, it: e.tensor_tensor(zc[:, :], zcur[:, :].broadcast_to([P, CAND]), cand_bits[:, i, :], ALU.bitwise_xor),
                  after=[before], key=("r_zc", i))
            route(lambda e, it: e.tensor_scalar(sgn[:, :], zc[:, :], 31, 1, ALU.arith_shift_right, ALU.logical_shift_right),
                  after=[("r_zc", i)], key=("r_sg", i))
            route(lambda e, it: e.tensor_tensor(thr[:, :], zc[:, :], sgn[:, :], ALU.bitwise_xor),
                  after=[("r_sg", i)], key=("r_th", i))
            route(lambda e, it: e.tensor_tensor(
                ge[:, :, :], k["scores"][:, bass.ds(it, 1), :].broadcast_to([P, CAND, NT]),
                thr[:, :].bitcast(F32).unsqueeze(2).broadcast_to([P, CAND, NT]), ALU.is_ge),
                after=[("r_th", i)], key=("r_ge", i))
            route(lambda e, it: e.tensor_reduce(part_cnt[:, :], ge[:, :, :], AX.X, ALU.add),
                  after=[("r_ge", i)], key=("r_pc", i))

        def bits_answer(i):
            route(lambda e, it: e.matmul(R[:, 0:CAND], ones_h[:, :], part_cnt[:, :], start=True, stop=True),
                  "tensor", [("r_pc", i)], ("r_cnt", i))
            route(lambda e, it: e.tensor_scalar(gem[:, :], R[:, 0:CAND], float(C), None, ALU.is_ge, ALU.add, accum_out=digit[:, :]),
                  after=[("r_cnt", i)], key=("r_dg", i))
            route(lambda e, it: e.tensor_scalar(zadd[:, :], digit[:, :], steps_f[:, i:i + 1], None, ALU.mult),
                  after=[("r_dg", i)], key=("r_za", i))
            route(lambda e, it: e.tensor_tensor(zcur[:, :], zcur[:, :], zadd[:, :].bitcast(I32), ALU.bitwise_xor),
                  after=[("r_za", i)], key=("r_z", i))

        def ranks(src, after, key):
            def fn(e, it):
                e.matmul(R[:, NT:2 * NT], below[:, :], src[:, :], start=True, stop=True)
                return e.matmul(R[:, 2 * NT:3 * NT], ones_h[:, :], src[:, :], start=True, stop=True)
            route(fn, "tensor", after, (key, "mm"))

        def rank_rows(key):
            route(lambda e, it: e.tensor_copy(cols[:, :], R[:, 2 * NT:3 * NT]), after=[(key, "mm")], key=(key, "col"))
            route(lambda e, it: e.tensor_tensor_scan(csum[:, :], cols[:, :], zero[:, :], 0.0, ALU.add, ALU.add),
                  after=[(key, "col")], key=(key, "scan"))
            route(lambda e, it: e.tensor_tensor(csum[:, :], csum[:, :], cols[:, :], ALU.subtract),
                  after=[(key, "scan")], key=(key, "before"))

        def choose():
            last = STEPS - 1
            route(lambda e, it: e.tensor_scalar(sgn[:, 0:1], zcur[:, :], 31, 1, ALU.arith_shift_right, ALU.logical_shift_right),
                  after=[("r_z", last)], key=("c_sg",))
            route(lambda e, it: e.tensor_tensor(thr[:, 0:1], zcur[:, :], sgn[:, 0:1], ALU.bitwise_xor), after=[("c_sg",)], key=("c_th",))

            def flags(dst, op):
                return lambda e, it: e.tensor_tensor(dst[:, :], k["scores"][:, bass.ds(it, 1), :].rearrange("p o t -> p (o t)"),
                                                     thr[:, 0:1].bitcast(F32).broadcast_to([P, NT]), op)
            route(flags(gt, ALU.is_gt), after=[("c_th",)], key=("c_gt",))
            route(flags(eq, ALU.is_equal), key=("c_eq",))
            route(lambda e, it: e.tensor_reduce(gt_cnt[:, :], gt[:, :], AX.X, ALU.add), after=[("c_gt",)], key=("c_gc",))

        def missing():
            route(lambda e, it: e.matmul(R[:, 0:1], ones_h[:, :], gt_cnt[:, :], start=True, stop=True), "tensor", [("c_gc",)], ("c_gn",))
            route(lambda e, it: e.tensor_scalar(need[:, :], R[:, 0:1], -1.0, float(C), ALU.mult, ALU.add), after=[("c_gn",)], key=("c_need",))

        def ties():
            ranks(eq, [("c_eq",), ("c_need",)], "tie")

        def choose_ties():
            rank_rows("tie")
            route(lambda e, it: e.tensor_tensor(rank[:, :], R[:, NT:2 * NT], csum[:, :], ALU.add), after=[("tie", "before")], key=("c_rank",))
            route(lambda e, it: e.scalar_tensor_tensor(tie[:, :], rank[:, :], need[:, 0:1], eq[:, :], ALU.is_lt, ALU.mult),
                  after=[("c_rank",)], key=("c_tie",))
            route(lambda e, it: e.tensor_tensor(sel[:, :], gt[:, :], tie[:, :], ALU.add), after=[("c_tie",)], key=("c_sel",))
            route(lambda e, it: e.tensor_copy(sel_i[:, :], sel[:, :]), after=[("c_sel",)], key=("c_seli",))

        def place():
            rank_rows("slot")
            route(lambda e, it: e.tensor_tensor(rank2[:, :], R[:, NT:2 * NT], csum[:, :], ALU.add), after=[("slot", "before")], key=("p_rank",))
            route(lambda e, it: e.scalar_tensor_tensor(rank2[:, :], rank2[:, :], base[:, 0:1], sel[:, :], ALU.add, ALU.mult),
                  after=[("p_rank",)], key=("p_slot",))
            route(lambda e, it: e.tensor_tensor(slot[:, :], slot[:, :], rank2[:, :], ALU.add), after=[("p_slot",)], key=("p_sum",))
            route(lambda e, it: e.tensor_scalar(base[:, :], base[:, :], float(C), None, ALU.add), key=("p_base",))
            ph.apart.add(("r_taken",))
            route(lambda e, it: e.copy_predicated(
                k["scores"][:, :, :], sel_i[:, :].unsqueeze(1).broadcast_to([P, E, NT]),
                lowest[:, :].unsqueeze(1).broadcast_to([P, E, NT])),
                after=[("p_base",)], key=("r_taken",))

        def unit(u, stage, at):
            return [(at, lambda: project("q", u, stage)), (at + 1, lambda: project("k", u, stage)),
                    (at + 2, lambda: rms("q", u, stage)), (at + 3, lambda: rms("k", u, stage)),
                    (at + 4, lambda: parts("q", u, stage)), (at + 4, lambda: project_v(u, stage)),
                    (at + 5, lambda: parts("k", u, stage))]

        work = unit(1, 1, 0) + unit(0, 0, 8) + [
            (1, lambda: normalise(3, 2)), (3, lambda: turn_o(0)), (4, lambda: turn_o(1)),
            (5, lambda: project_o(0)), (6, lambda: project_o(1)),
            (4, load_x), (5, norm_x), (6, lambda: turn_x(0)), (7, lambda: turn_x(1)),
            (7, lambda: normalise(0)), (11, lambda: normalise(1)), (15, lambda: normalise(2))]
        ask = {i: (lambda i=i: bits_ask(i)) for i in range(STEPS)}
        answer = {i: (lambda i=i: bits_answer(i)) for i in range(STEPS)}
        ask[STEPS], answer[STEPS] = choose, missing
        answer[STEPS + 1] = ties
        ask[STEPS + 2] = choose_ties
        answer[STEPS + 2] = lambda: ranks(sel, [("c_sel",)], "slot")
        ask[STEPS + 3] = place

        for s in range(8):
            if s % 4 == 0:
                shift(s // 4)
            for half in range(2):
                point = 2 * s + half
                ask.get(point, lambda: None)()
                heads(s, 2 * half)
                heads(s, 2 * half + 1)
                if s:
                    weigh(s - 1, half)
                for at, fn in work:
                    if at == point:
                        fn()
                answer.get(point, lambda: None)()
        weigh(7, 0)
        weigh(7, 1)
        assert len(job_release) % 2 == 0 and job_release[-2:] == job_release_tail, job_release

        with nc.Block() as block:
            def program_for(eng):
                def program(e):
                    if eng in ("tensor", "vector", "sync"):
                        needed[eng] = e.value_load(flag[0:1, 0:1], min_val=0, max_val=1)
                    for its, stages, groups in plan:
                        if isinstance(its, int):
                            ph.body(eng, e, its, stages, groups)
                        else:
                            with e.Fori(its[0], its[1]) as it:
                                ph.body(eng, e, it, stages, groups)
                return program
            both, rest = {"", "route"}, {""}
            plan = [(-1, {0}, both), (0, {0, 1}, both), ((1, E), {0, 1, 2}, both),
                    ((E, B - 1), {0, 1, 2}, rest), (B - 1, {1, 2}, rest), (B, {2}, rest)]
            for eng in ("sync", "scalar", "vector", "gpsimd", "tensor"):
                on_engine(block, eng)(program_for(eng))

        s_o = [ctx.enter_context(nc.semaphore(f"o_{i}")) for i in range(2)]
        with nc.Block() as block:
            @block.vector
            def _(e):
                e.tensor_copy(k["slot_i"][:, :], slot[:, :]).then_inc(s_o[0], 1)

            @block.gpsimd
            def _(e):
                e.wait_ge(s_o[0], 1)
                for t in range(NT):
                    e.indirect_dma_start(out=order_dram, out_offset=bass.IndirectOffsetOnAxis(ap=k["slot_i"][:, t:t + 1], axis=0),
                                         in_=k["tokens"][:, t:t + 1], in_offset=None).then_inc(s_o[1], 16)
                e.wait_ge(s_o[1], 16 * NT)


def experts(nc, a, x_rows, attn_dram, order_dram, out, k):
    U = 2
    assert C == U * N
    with ExitStack() as ctx:
        def sb(name, shape, dt=F32):
            return ctx.enter_context(nc.sbuf_tensor(name, shape, dt))

        w1raw = sb("w1raw", [P, KD, F])
        w2raw = sb("w2raw", [P, NFC, D])
        w1 = [sb(f"w1_{i}", [P, KD, F], F32R) for i in range(2)]
        w2 = [sb(f"w2_{i}", [P, NFC, D], F32R) for i in range(2)]
        b1 = sb("b1", [P, E, NFC])
        b2 = sb("b2", [P, E, D])
        order = sb("order_s", [P, E, U, CH], I32)
        rows = [sb(f"rows{u}", [P, CH], I32) for u in range(U)]
        rows_in = [sb(f"rows_in{u}", [P, CH], I32) for u in range(U)]
        gx = [sb(f"gx{u}", [P, CH, D]) for u in range(U)]
        ga = [sb(f"ga{u}", [P, CH, D]) for u in range(U)]
        xn = sb("e_xn", [P, CH, D])
        z = sb("e_z", [P, CH, D])
        base = [sb(f"base{u}", [P, CH, D]) for u in range(U)]
        nf = sb("nf", [P, KD, N])
        nT = [[sb(f"nT{u}{i}", [P, KD, N], F32R) for i in range(2)] for u in range(U)]
        act = [sb(f"act{i}", [P, N]) for i in range(2)]
        hid = [sb(f"hid{i}", [P, NFC, N], F32R) for i in range(2)]
        y = [sb(f"y{u}", [P, CH, D]) for u in range(U)]
        stt = [[sb(f"e_{n}{i}", s) for n, s in (("st", [P, CH, 6]), ("mv", [P, CH, 2]), ("ve", [P, CH]), ("rs", [P, CH]))]
               for i in range(2)]
        up = [ctx.enter_context(nc.psum_tensor(f"up{i}", [P, N], F32)) for i in range(2)]
        turned = [ctx.enter_context(nc.psum_tensor(f"tu{i}", [P, N], F32)) for i in range(KD)]
        down = [ctx.enter_context(nc.psum_tensor(f"dn{c}", [P, N], F32)) for c in range(CH)]
        PRODUCTS = ((0, 0), (0, 1), (1, 0))

        s_c = ctx.enter_context(nc.semaphore("e_c"))
        with nc.Block() as block:
            @block.sync
            def _(e):
                loads = [(b1[:, :, :], a["b1"]), (b2[:, :, :].rearrange("p e d -> p (e d)"),
                          a["b2"].rearrange("(o e) d -> o (e d)", o=1).broadcast_to([P, E * D])),
                         (order[:, :, :, :].rearrange("p e u c -> p (e u c)"), order_dram.rearrange("(t p) o -> p (t o)", p=P))]
                for dst, src in loads:
                    e.dma_start(dst, src, allow_slow_non_contiguous=True).then_inc(s_c, 16)
                e.wait_ge(s_c, 16 * len(loads))

        ph = Phase(nc, "e", ctx, 1)

        def ex(it, stage):
            return it + 1 - stage

        def load_weights(name, raw, src):
            ph.dma("sync", [lambda e, it: e.dma_start(raw[:, :, :], src[ex(it, 0)])], [("prev", (name, "lo"))], (name, "raw"), 0)

        def split(name, raw, parts, last_use):
            ph.op("scalar", lambda e, it: e.activation(parts[0][:, :, :], raw[:, :, :], ACT.Copy),
                  [(name, "raw"), last_use], (name, "hi"), 0)
            ph.op("vector", lambda e, it: e.tensor_tensor(parts[1][:, :, :], raw[:, :, :], parts[0][:, :, :].bitcast(F32), ALU.subtract),
                  [(name, "hi")], (name, "lo"), 0)

        def gather(u):
            ph.op("gpsimd", lambda e, it: e.tensor_copy(rows_in[u][:, :], order[:, bass.ds(ex(it, 0), 1), u, :].rearrange("p o c -> p (o c)")),
                  [("rows", u) if u else ("prev", ("rows", u))], ("rows_in", u), 0)
            fns = [lambda e, it, c=c, dst=dst, src=src: e.indirect_dma_start(
                out=dst[:, c, :], out_offset=None, in_=src,
                in_offset=bass.IndirectOffsetOnAxis(ap=rows_in[u][:, c:c + 1], axis=0))
                for c in range(CH) for dst, src in ((gx[u], x_rows), (ga[u], attn_dram))]
            ph.dma("gpsimd", fns, [("rows_in", u), ("base", u) if u else ("prev", ("base", u))], ("gather", u), 0)

        def prepare(u, stage):
            tag = f"g{u}"
            gathered = ("prev", ("gather", 1)) if u else ("gather", 0)

            def other(*step):
                return ("prev", step) if u else step
            one = LayerNorm(ph, tag, gx[u], stt[0], k, xn, stage)
            one.moments([gathered])
            one.scale([other("base", 1 - u)])
            ph.op("gpsimd", lambda e, it: e.tensor_copy(rows[u][:, :], rows_in[u][:, :]),
                  [gathered, other("scatter", u)], ("rows", u), stage)
            ph.op("vector", lambda e, it: e.tensor_tensor(ga[u][:, :, :], ga[u][:, :, :], gx[u][:, :, :], ALU.add),
                  [gathered], ("xa", u), stage)
            ph.op("vector", lambda e, it: e.tensor_tensor(base[u][:, :, :], ga[u][:, :, :], xn[:, :, :], ALU.add),
                  [("xa", u), (tag, "out"), other("y", u, CH - 1)], ("base", u), stage)
            two = LayerNorm(ph, tag + "n", xn, stt[1], k, z, stage)
            two.moments([(tag, "out")])
            two.scale([other("turn", 1 - u, KD - 1)])

        def turn(u, stage):
            def other(*step):
                return ("prev", step) if u else step
            for d in range(KD):
                def fn(e, it, d=d):
                    for c in range(CH):
                        ins = e.transpose(turned[d][:, c * P:(c + 1) * P], z[:, c, d * P:(d + 1) * P], k["ident"][:, :])
                    return ins
                ph.op("tensor", fn, [(f"g{u}n", "out"), other("affine", 1 - u, d)], ("turn", u, d), stage)
                ph.op("vector", lambda e, it, d=d: e.tensor_scalar(nf[:, d, :], turned[d][:, :], k["gain"][:, d:d + 1],
                                                                  k["offset"][:, d:d + 1], ALU.mult, ALU.add),
                      [("turn", u, d), other("nlo", 1 - u, d)], ("affine", u, d), stage)
                ph.op("scalar", lambda e, it, d=d: e.activation(nT[u][0][:, d, :], nf[:, d, :], ACT.Copy),
                      [("affine", u, d), other("up", u, NFC - 1)], ("nhi", u, d), stage)
                ph.op("gpsimd", lambda e, it, d=d: e.tensor_tensor(nT[u][1][:, d, :], nf[:, d, :], nT[u][0][:, d, :].bitcast(F32), ALU.subtract),
                      [("nhi", u, d)], ("nlo", u, d), stage)

        def layer_up(u, fc):
            def before(name, back):
                i = (NFC * u + fc) - back
                step = (name, i // NFC % 2, i % NFC)
                return ("prev", step) if i < 0 else step

            def fn(e, it):
                for i, (d, (pw, px)) in enumerate((d, pr) for d in range(KD) for pr in PRODUCTS):
                    ins = e.matmul(up[fc % 2][:, :], w1[pw][:, d, fc * P:(fc + 1) * P], nT[u][px][:, d, :],
                                   start=(i == 0), stop=(i == KD * len(PRODUCTS) - 1))
                return ins
            ready = ("nlo", u, KD - 1) if u else ("prev", ("nlo", u, KD - 1))
            ph.op("tensor", fn, [("prev", ("w1", "lo")), ready, before("gelu", 2)], ("up", u, fc))
            ph.apart.add(("gelu", u, fc))
            ph.op("scalar", lambda e, it: e.activation(act[fc % 2][:, :], up[fc % 2][:, :], ACT.Gelu_apprx_tanh,
                                                       bias=b1[:, bass.ds(it, 1), fc:fc + 1].rearrange("p o c -> p (o c)")),
                  [("up", u, fc), before("hlo", 2)], ("gelu", u, fc))
            ph.op("scalar", lambda e, it: e.activation(hid[0][:, fc, :], act[fc % 2][:, :], ACT.Copy),
                  [("gelu", u, fc), before("down", NFC)], ("hhi", u, fc))
            ph.op("vector", lambda e, it: e.tensor_tensor(hid[1][:, fc, :], act[fc % 2][:, :], hid[0][:, fc, :].bitcast(F32), ALU.subtract),
                  [("hhi", u, fc)], ("hlo", u, fc))

        def layer_down(u, fc):
            for c in range(CH):
                def fn(e, it, c=c):
                    for i, (ph_, pw) in enumerate(PRODUCTS):
                        ins = e.matmul(down[c][:, 0:D], hid[ph_][:, fc, c * P:(c + 1) * P], w2[pw][:, fc, :],
                                       start=(fc == 0 and i == 0), stop=(fc == NFC - 1 and i == len(PRODUCTS) - 1))
                    return ins
                after = [("hlo", u, fc), ("prev", ("w2", "lo"))]
                if fc == 0:
                    after.append(("t", 0, c) if u else ("prev", ("t", 1, c)))
                key = ("down_c", u, c) if fc == NFC - 1 and c < CH - 1 else ("down", u, fc) if c == CH - 1 else None
                ph.op("tensor", fn, after, key)

        def finish(u):
            for c in range(CH):
                ph.op("vector", lambda e, it, c=c: e.tensor_tensor(
                    y[u][:, c, :], down[c][:, 0:D], b2[:, bass.ds(it, 1), :].rearrange("p o d -> p (o d)"), ALU.add),
                    [("down_c", u, c) if c < CH - 1 else ("down", u, NFC - 1), ("prev", ("scatter", u))], ("t", u, c))
                base_of = ("base", u) if u else ("prev", ("base", u))
                ph.op("vector", lambda e, it, c=c: e.tensor_tensor(y[u][:, c, :], y[u][:, c, :], base[u][:, c, :], ALU.add),
                      [("t", u, c), base_of], ("y", u, c))
            ph.dma("gpsimd", [lambda e, it, c=c: e.indirect_dma_start(
                out=out, out_offset=bass.IndirectOffsetOnAxis(ap=rows[u][:, c:c + 1], axis=0),
                in_=y[u][:, c, :], in_offset=None) for c in range(CH)],
                [("y", u, CH - 1), ("rows", u) if u else ("prev", ("rows", u))], ("scatter", u))

        load_weights("w1", w1raw, a["w1"])
        load_weights("w2", w2raw, a["w2"])
        gather(0)
        for u in range(U):
            stage = 1 if u == 0 else 0
            for fc in range(NFC):
                layer_up(u, fc)
                if fc == 0:
                    prepare(1 - u, stage)
                    if u == 0:
                        gather(1)
                if fc == NFC - 3:
                    turn(1 - u, stage)
            if u == 1:
                split("w1", w1raw, w1, ("up", 1, NFC - 1))
            for fc in range(NFC):
                layer_down(u, fc)
            finish(u)
        split("w2", w2raw, w2, ("down", 1, NFC - 1))
        run_phase(nc, ph, ["sync", "gpsimd", "vector", "scalar", "tensor"],
                  [(-1, {0}, {""}), (0, {0, 1}, {""}), ((1, E - 1), {0, 1}, {""}), (E - 1, {1}, {""})])
        with nc.Block() as block:
            @block.sync
            def _(e):
                for u in range(U):
                    e.wait_ge(*ph.value(("scatter", u), E - 1))


def kernel(**inputs):
    import concourse.bacc as bacc
    from concourse.bass_utils import run_bass_kernel_spmd

    def on_partitions(w):
        return w.reshape(-1, P, w.shape[-1]).transpose(1, 0, 2)

    i = {n: np.asarray(v) for n, v in inputs.items()}
    row, col = np.arange(P)[:, None], np.arange(P)[None, :]
    shifts = [BITS * s for s in range(STEPS)][::-1]
    beyond = 0xff7fffff
    cand = np.array([[(c + 1) << s if (c + 1) << s < 2 ** 32 else beyond for c in range(CAND)] for s in shifts],
                    np.uint32).view(np.int32)
    arrays = {
        "x": i["L0_attn_x"],
        "wq": on_partitions(i["L0_attn_Wq"].T), "wk": on_partitions(i["L0_attn_Wk"].T),
        "wv": on_partitions(i["L0_attn_Wv"].T), "wo": on_partitions(i["L0_attn_Wo"].T),
        "qk_w": np.stack([np.tile(i["L0_attn_qn_w"], HU), np.tile(i["L0_attn_kn_w"], HU)], 1),
        "centroids": on_partitions(i["L0_ffn_centroids"].T),
        "ln_g": i["L0_ffn_ln_g"].reshape(KD, P).T, "ln_b": i["L0_ffn_ln_b"].reshape(KD, P).T,
        "w1": i["L0_ffn_w1"].reshape(E, KD, P, F).transpose(0, 2, 1, 3),
        "w2": i["L0_ffn_w2"].reshape(E, NFC, P, D).transpose(0, 2, 1, 3),
        "b1": i["L0_ffn_b1"].reshape(E, NFC, P).transpose(2, 0, 1),
        "b2": i["L0_ffn_b2"],
        "ident": np.eye(P, dtype=np.float32),
        "headsum": (row // DH == col // DH).astype(np.float32),
        "tokens": (np.arange(NT)[None, :] * P + np.arange(P)[:, None]).astype(np.int32),
        "cand_bits": np.broadcast_to(cand[None], (P, STEPS, CAND)),
        "steps_f": np.broadcast_to(np.array([2.0 ** s for s in shifts], np.float32)[None], (P, STEPS)),
    }
    nc = bacc.Bacc("TRN2", target_bir_lowering=False, num_devices=1)
    maps, aps = {}, {}
    for name, v in arrays.items():
        v = np.ascontiguousarray(v)
        maps[f"in_{name}"] = v
        aps[name] = nc.dram_tensor(f"in_{name}", v.shape, mybir.dt.from_np(v.dtype), kind="ExternalInput").ap()
    out = nc.dram_tensor("out", (T, D), F32, kind="ExternalOutput").ap()
    build(nc, aps, out)
    r = run_bass_kernel_spmd(nc, [maps], core_ids=[0])
    return r.results[0]["out"].reshape(B, N, D)
```

```python
import numpy as np
import concourse.bass as bass
from concourse import mybir
from contextlib import ExitStack

F32 = mybir.dt.float32
F32R = mybir.dt.float32r
BF16 = mybir.dt.bfloat16
I32 = mybir.dt.int32
U32 = mybir.dt.uint32
ALU = mybir.AluOpType
ACT = mybir.ActivationFunctionType
AX = mybir.AxisListType

B, N, D = 16, 512, 256
H, DH = 16, 16
E, F = 8, 1024
T = B * N
C = T // E
P = 128
NT = T // P
CH = N // P
KD = D // P
HU = P // DH
NFC = F // P
LN_EPS = 1e-5
RMS_EPS = float(np.finfo(np.float32).eps)
SCALE = DH ** -0.5
ROW_SHIFT, ROWS = 64, 96
SAFE_BOUND = 60.0
BITS = 3
STEPS = -(-32 // BITS)
CAND = 2 ** BITS - 1


class Phase:

    def __init__(self, nc, name, ctx, last_stage):
        self.nc, self.name, self.ctx, self.last = nc, name, ctx, last_stage
        self.queue, self.where, self.sems, self.per = {}, {}, {}, {}
        self.first = {}
        self.apart = set()

    def sem(self, name):
        if name not in self.sems:
            self.sems[name] = self.ctx.enter_context(self.nc.semaphore(f"{self.name}_{name}"))
            self.per[name] = 0
        return name

    def op(self, eng, fn, after=(), key=None, stage=1, group=""):
        if key is not None:
            s = self.sem(f"{eng}{group}")
            self.per[s] += 1
            assert key not in self.where, key
            self.where[key] = (s, self.per[s])
        self.queue.setdefault(eng, []).append((fn, tuple(after), key, stage, group, 1))

    def dma(self, eng, fns, after=(), key=None, stage=1, group=""):
        s = self.sem("dma_" + "_".join(map(str, key)) if isinstance(key, tuple) else f"dma_{key}")
        self.per[s] += 16 * len(fns)
        self.where[key] = (s, self.per[s])
        if eng == "gpsimd":
            self.first[s] = stage - 1

        def issue(e, it):
            for f in fns:
                f(e, it).then_inc(self.sems[s], 16)
            return None
        self.queue.setdefault(eng, []).append((issue, tuple(after), key, stage, group, 16 * len(fns)))

    def value(self, step, it):
        s, k = self.where[step]
        return self.sems[s], (it - self.first.get(s, -1)) * self.per[s] + k

    def wait(self, e, after, it, apart):
        for a in after:
            back = 0
            if a[0] == "prev":
                back, a = 1, a[1]
            if back and isinstance(it, int) and self.value(a, it - back)[1] <= 0:
                continue
            e.wait_ge(*self.value(a, it - back))
            if apart and not isinstance(it, int):
                e.nop(nofuse=True)

    def body(self, eng, e, it, stages, groups):
        skipped = {}
        waited = {}

        def settle():
            for s, n in skipped.items():
                e.drain()
                e.sem_inc(self.sems[s], n)
            skipped.clear()

        for fn, after, key, stage, group, n in self.queue.get(eng, []):
            if stage not in stages or group not in groups:
                name = self.where[key][0] if key else ""
                over = not key or name in self.first or (name.startswith("dma_") and stage < min(stages))
                if not over and group in groups:
                    s = self.where[key][0]
                    skipped[s] = skipped.get(s, 0) + n
                continue
            settle()
            need = []
            for a in after:
                back, b = (1, a[1]) if a[0] == "prev" else (0, a)
                if b not in self.where:
                    raise KeyError(b)
                s, k = self.where[b]
                if waited.get(s, (-9, 0)) < (-back, k):
                    waited[s] = (-back, k)
                    need.append(a)
            self.wait(e, need, it, eng in ("gpsimd", "sync") or key in self.apart)
            ins = fn(e, it)
            if key is not None and ins is not None:
                ins.then_inc(self.sems[self.where[key][0]], 1)
        settle()


def on_engine(block, eng):
    return {"sync": block.sync, "scalar": block.scalar, "vector": block.vector,
            "gpsimd": block.gpsimd, "tensor": block.tensor}[eng]


def run_phase(nc, phase, engines, plan):
    with nc.Block() as block:
        for eng in engines:
            def program(e, eng=eng):
                for its, stages, groups in plan:
                    if isinstance(its, int):
                        phase.body(eng, e, its, stages, groups)
                    elif any(x[3] in stages and x[4] in groups for x in phase.queue.get(eng, [])):
                        with e.Fori(its[0], its[1]) as it:
                            phase.body(eng, e, it, stages, groups)
            on_engine(block, eng)(program)


def build(nc, a, out):
    x_batch = a["x"].rearrange("b (c p) d -> b p c d", p=P)
    rows_dram = nc.dram_tensor("rows", (T, 2 * D), F32, kind="Internal").ap()
    order_dram = nc.dram_tensor("order", (T, 1), I32, kind="Internal").ap()
    parts_dram = nc.dram_tensor("parts", (2, 2, 2, P, N), F32, kind="Internal").ap()
    shift_dram = nc.dram_tensor("shifts", (2, HU * CH, P), F32, kind="Internal").ap()

    with ExitStack() as top:
        def sb(name, shape, dt, ctx=top):
            return ctx.enter_context(nc.sbuf_tensor(name, shape, dt))

        k = {}
        k["ident"] = sb("ident", [P, P], F32)
        k["gain"] = sb("gain", [P, KD], F32)
        k["offset"] = sb("offset", [P, KD], F32)
        k["eps_ln"] = sb("eps_ln", [P, CH], F32)
        k["half"] = sb("half", [P, CH], F32)
        k["minus"] = sb("minus", [P, CH], F32)
        k["mean"] = sb("mean", [P, NT], F32)
        k["rstd"] = sb("rstd", [P, NT], F32)
        k["tokens"] = sb("tokens", [P, NT], I32)
        with ExitStack() as mid:
            k["scores"] = sb("scores", [P, E, NT], F32, mid)
            statistics_and_scores(nc, a, x_batch, k)
            attention_and_routing(nc, a, x_batch, rows_dram, order_dram, parts_dram, shift_dram, k)
        experts(nc, a, rows_dram, order_dram, out, k)


class LayerNorm:

    def __init__(self, ph, tag, src, tiles, k, dst, stage):
        self.ph, self.tag, self.src, self.k, self.dst, self.stage = ph, tag, src, k, dst, stage
        self.stats, self.aggr, self.veps, self.rstd = tiles

    def moments(self, after, free_aggr=()):
        ph, tag, stage, k = self.ph, self.tag, self.stage, self.k

        def stat(e, it):
            for c in range(CH):
                ins = e.bn_stats(self.stats[:, c, :], self.src[:, c, :])
            return ins
        ph.op("vector", stat, after, (tag, "stat"), stage)

        def agg(e, it):
            for c in range(CH):
                ins = e.bn_aggr(self.aggr[:, c, :], self.stats[:, c, :])
            return ins
        ph.apart.add((tag, "agg"))
        ph.op("vector", agg, [(tag, "stat"), *free_aggr], (tag, "agg"), stage)
        ph.op("gpsimd", lambda e, it: e.tensor_tensor(self.veps[:, :], self.aggr[:, :, 1], k["eps_ln"][:, :], ALU.add),
              [(tag, "agg")], (tag, "veps"), stage)
        ph.op("gpsimd", lambda e, it: e.tensor_tensor(self.rstd[:, :], self.veps[:, :], k["half"][:, :], ALU.pow),
              [(tag, "veps")], (tag, "rstd"), stage)

    def scale(self, free_dst=()):
        def fn(e, it):
            for c in range(CH):
                ins = e.tensor_scalar(self.dst[:, c, :], self.src[:, c, :], self.aggr[:, c, 0:1],
                                      self.rstd[:, c:c + 1], ALU.subtract, ALU.mult)
            return ins
        self.ph.op("vector", fn, [(self.tag, "rstd"), *free_dst], (self.tag, "out"), self.stage)


def statistics_and_scores(nc, a, x_batch, k):
    with ExitStack() as ctx:
        def sb(name, shape, dt):
            return ctx.enter_context(nc.sbuf_tensor(name, shape, dt))

        cent = sb("cent", [P, KD, E], F32)
        xb = [sb(f"s_x{r}", [P, CH, D], F32) for r in range(2)]
        xn = [sb(f"s_xn{r}", [P, CH, D], F32) for r in range(2)]
        z = [sb(f"s_z{r}", [P, CH, D], F32) for r in range(2)]
        normT = [sb(f"s_nT{r}", [P, KD, N], F32) for r in range(2)]
        small = [[sb(f"s_{n}{r}{i}", s, F32) for n, s in
                  (("st", [P, CH, 6]), ("mv", [P, CH, 2]), ("ve", [P, CH]), ("rs", [P, CH]))]
                 for r in range(2) for i in range(2)]
        turned = [[ctx.enter_context(nc.psum_tensor(f"s_t{r}{d}", [P, N], F32)) for d in range(KD)]
                  for r in range(2)]
        score = [ctx.enter_context(nc.psum_tensor(f"s_s{r}", [P, CH, E], F32)) for r in range(2)]
        s_const, s_pool = (ctx.enter_context(nc.semaphore(n)) for n in ("s_const", "s_pool"))

        with nc.Block() as block:
            @block.sync
            def _(e):
                loads = [(k["ident"][:, :], a["ident"]), (k["gain"][:, :], a["ln_g"]),
                         (k["offset"][:, :], a["ln_b"]), (k["tokens"][:, :], a["tokens"]),
                         (cent[:, :, :], a["centroids"])]
                for dst, src in loads:
                    e.dma_start(dst, src).then_inc(s_const, 16)
                e.wait_ge(s_const, 16 * len(loads))

            @block.gpsimd
            def _(e):
                e.memset(k["eps_ln"][:, :], LN_EPS)
                e.memset(k["minus"][:, :], -1.0)
                e.memset(k["half"][:, :], -0.5).then_inc(s_pool, 1)
                e.wait_ge(s_pool, 1)

        ph = Phase(nc, "s", ctx, 2)
        R2 = range(2)

        def first(it, r, stage):
            return CH * (2 * (it + 1 - stage) + r)

        norm = [[LayerNorm(ph, f"a{r}", xb[r], small[2 * r], k, xn[r], 0),
                 LayerNorm(ph, f"b{r}", xn[r], small[2 * r + 1], k, z[r], 1)] for r in R2]
        for r in R2:
            ph.dma("sync", [lambda e, it, r=r: e.dma_start(xb[r][:, :, :], x_batch[2 * (it + 1) + r])],
                   [("prev", (f"a{r}", "out"))], ("x", r), 0)
        for r in R2:
            for d in range(KD):
                def turn(e, it, r=r, d=d):
                    for c in range(CH):
                        ins = e.transpose(turned[r][d][:, c * P:(c + 1) * P],
                                          z[r][:, c, d * P:(d + 1) * P], k["ident"][:, :])
                    return ins
                ph.op("tensor", turn, [("prev", (f"b{r}", "out")), ("prev", ("gain", r, d))], ("turn", r, d), 2)
                ph.op("scalar", lambda e, it, r=r, d=d: e.activation(
                    normT[r][:, d, :], turned[r][d][:, :], ACT.Identity, bias=k["offset"][:, d:d + 1],
                    scale=k["gain"][:, d:d + 1]), [("turn", r, d), ("prev", ("score", r))], ("gain", r, d), 2)
        for r in R2:
            def score_mm(e, it, r=r):
                for c in range(CH):
                    for d in range(KD):
                        ins = e.matmul(score[r][:, c, :], normT[r][:, d, c * P:(c + 1) * P],
                                       cent[:, d, :], start=(d == 0), stop=(d == KD - 1))
                return ins
            ph.op("tensor", score_mm, [("gain", r, KD - 1), ("prev", ("keep", r))], ("score", r), 2)
        for r in R2:
            norm[r][1].moments([("prev", (f"a{r}", "out"))])
        for r in R2:
            norm[r][0].moments([("x", r)], [("prev", (f"kept{r}",))])
        for r in R2:
            norm[r][1].scale([("turn", r, KD - 1)])
        for r in R2:
            norm[r][0].scale([(f"b{r}", "out")])

            def keep(e, it, r=r):
                at = bass.ds(first(it, r, 0), CH)
                e.tensor_copy(k["rstd"][:, at], norm[r][0].rstd[:, :])
                return e.tensor_copy(k["mean"][:, at], norm[r][0].aggr[:, :, 0])
            ph.op("gpsimd", keep, [(f"a{r}", "rstd")], (f"kept{r}",), 0)
        for r in R2:
            ph.op("vector", lambda e, it, r=r: e.tensor_copy(
                k["scores"][:, :, bass.ds(first(it, r, 2), CH)].rearrange("p e c -> p c e"), score[r][:, :, :]),
                [("score", r)], ("keep", r), 2)
        n = B // 2
        run_phase(nc, ph, ["sync", "vector", "gpsimd", "tensor", "scalar"],
                  [(-1, {0}, {""}), (0, {0, 1}, {""}), ((1, n - 1), {0, 1, 2}, {""}), (n - 1, {1, 2}, {""}), (n, {2}, {""})])


def split_weights(nc, ctx, block, jobs, raw, sem_load, sem_hi, sem_lo):
    @block.sync
    def _(e):
        for (src, _, _), land in zip(jobs, raw):
            e.dma_start(land[:, :, :], src).then_inc(sem_load, 16)
        e.wait_ge(sem_load, 16 * len(jobs))

    @block.scalar
    def _(e):
        e.preload_act_table_set("natural_log_exp_and_others")
        e.wait_ge(sem_load, 16 * len(jobs))
        for (_, hi, _), land in zip(jobs, raw):
            e.activation(hi[:, :, :], land[:, :, :], ACT.Copy).then_inc(sem_hi, 1)

    @block.vector
    def _(e):
        for i, ((_, hi, lo), land) in enumerate(zip(jobs, raw)):
            e.wait_ge(sem_hi, i + 1)
            e.tensor_tensor(lo[:, :, :], land[:, :, :], hi[:, :, :].bitcast(F32), ALU.subtract).then_inc(sem_lo, 1)


def attention_and_routing(nc, a, x_batch, rows_dram, order_dram, parts_dram, shift_dram, k):
    G = 4
    VW = 32
    with ExitStack() as ctx:
        def sb(name, shape, dt):
            return ctx.enter_context(nc.sbuf_tensor(name, shape, dt))

        def ps(name, shape):
            return ctx.enter_context(nc.psum_tensor(name, shape, F32))

        ctx.enter_context(nc.allow_low_precision(reason="counts of at most NT tokens are exact in bfloat16"))
        w = {n: [sb(f"w{n}{i}", [P, KD, D], F32R) for i in range(2)] for n in "qkv"}
        wo = sb("wo", [P, KD, D], F32)
        headsum = sb("headsum", [P, P], F32)
        ones_h = sb("ones_h", [P, P], BF16)
        below = sb("below", [P, P], BF16)
        qk_w = sb("qk_w", [P, 2], F32)
        wq_scale = sb("wq_scale", [P, 1], F32)
        eps_rms = sb("eps_rms", [P, 1], F32)
        flag_f = sb("flag_f", [1, 2], F32)
        flag = sb("flag", [1, 1], I32)
        xb = sb("xb", [P, CH, D], F32)
        xn = sb("xn", [P, CH, D], F32)
        xT = [sb(f"xT{i}", [P, KD, N], F32R) for i in range(2)]
        raw = {n: sb(f"raw{n}", [P, N], F32) for n in "qk"}
        sq = {n: sb(f"sq{n}", [P, N], F32) for n in "qk"}
        inv = {n: sb(f"inv{n}", [P, N], F32) for n in "qk"}
        full = {n: sb(f"full{n}", [P, N], F32) for n in "qk"}
        part = {n: [sb(f"part{n}{i}", [P, N], F32R) for i in range(2)] for n in "qk"}
        stack = {n: [sb(f"stack{n}{u}", [ROWS, HU, N], F32R) for u in range(2)] for n in "qk"}
        v = [sb(f"v{u}", [P, CH, HU, VW], F32) for u in range(2)]
        v_next = sb("v_next", [P, CH, P], F32)
        prob = [sb(f"prob{i}", [P, G, 2, N], F32) for i in range(2)]
        oT = [sb(f"oT{i}", [P, N], F32) for i in range(2)]
        rden = [sb(f"rden{i}", [P, CH, G], F32) for i in range(2)]
        o_tok = sb("o_tok", [P, CH, D], F32)
        oT2 = sb("oT2", [P, KD, N], F32)
        xs = sb("xs", [P, CH, D], F32)
        ao = sb("ao", [P, CH, D], F32)
        mx = sb("mx", [P, HU * CH], F32)
        sh = [sb(f"sh{i}", [HU * CH, P], F32R) for i in range(2)]
        shf = sb("shf", [HU * CH, P], F32)
        cand_bits = sb("cand_bits", [P, STEPS, CAND], I32)
        steps_f = sb("steps_f", [P, STEPS], F32)
        zc = sb("zc", [P, CAND], I32)
        sgn = sb("sgn", [P, CAND], I32)
        thr = sb("thr", [P, CAND], I32)
        zcur = sb("zcur", [P, 1], I32)
        zadd = sb("zadd", [P, 1], U32)
        digit = sb("digit", [P, 1], F32)
        ge = sb("ge", [P, CAND, NT], F32)
        part_cnt = sb("part_cnt", [P, CAND], BF16)
        gem = sb("gem", [P, CAND], F32)
        gt = sb("gt", [P, NT], BF16)
        gt_cnt = sb("gt_cnt", [P, 1], BF16)
        eq = sb("eq", [P, NT], BF16)
        need = sb("need", [P, 1], F32)
        cols = sb("cols", [P, NT], F32)
        zero = sb("zero", [P, NT], F32)
        csum = sb("csum", [P, NT], F32)
        rank = sb("rank", [P, NT], F32)
        tie = sb("tie", [P, NT], F32)
        sel = sb("sel", [P, NT], BF16)
        sel_i = sb("sel_i", [P, NT], I32)
        rank2 = sb("rank2", [P, NT], F32)
        slot = sb("slot", [P, NT], F32)
        slot_i = sb("slot_i", [P, NT], I32)
        ORDERED = NT // (B - E)
        slot_now = sb("slot_now", [P, ORDERED], I32)
        token_now = sb("token_now", [P, ORDERED], I32)
        base = sb("base", [P, 1], F32)
        lowest = sb("lowest", [P, 1], F32)

        S = [ps(f"S{i}", [P, 2, N]) for i in range(2)]
        pv = ps("pv", [P, N])
        W = [ps(f"W{i}", [P, N]) for i in range(2)]
        R = ps("R", [P, N])

        sems = [ctx.enter_context(nc.semaphore(n)) for n in ("a_ld", "a_hi", "a_lo", "a_c", "a_v", "a_t", "a_p", "a_f")]
        s_ld, s_hi, s_lo, s_c, s_v, s_t, s_p, s_f = sems
        with nc.Block() as block:
            jobs = [(a[f"w{n}"], w[n][0], w[n][1]) for n in "qkv"]
            split_weights(nc, ctx, block, jobs, [t[:, 0:KD, :] for t in (xb, xn, o_tok)], s_ld, s_hi, s_lo)
        with nc.Block() as block:
            @block.sync
            def _(e):
                loads = [(wo[:, :, :], a["wo"]), (headsum[:, :], a["headsum"]), (qk_w[:, :], a["qk_w"]),
                         (cand_bits[:, :, :], a["cand_bits"]), (steps_f[:, :], a["steps_f"])]
                for dst, src in loads:
                    e.dma_start(dst, src).then_inc(s_c, 16)
                e.wait_ge(s_c, 16 * len(loads))

            @block.vector
            def _(e):
                done = 0
                for t, val in ((eps_rms, RMS_EPS), (lowest, float(np.finfo(np.float32).min)), (base, 0.0), (slot, 0.0), (zero, 0.0), (ones_h, 1.0)):
                    e.memset(t[:, :], val)
                for u in range(2):
                    e.memset(v[u][:, :, :, :], 1.0)
                    for n in "qk":
                        e.memset(stack[n][u][:, :, :].bitcast(F32), 0.0).then_inc(s_v, 1)
                        done += 1
                e.wait_ge(s_v, done)
                for u in range(2):
                    e.memset(stack["k"][u][ROW_SHIFT:ROW_SHIFT + 2, :, :].bitcast(F32), 1.0)
                e.wait_ge(s_c, 16 * 5)
                e.scalar_tensor_tensor(wq_scale[:, :], qk_w[:, 0:1], SCALE, qk_w[:, 1:2], ALU.mult, ALU.mult).then_inc(s_v, 1)
                e.wait_ge(s_t, 1)
                e.tensor_reduce(flag_f[:, 0:1], R[0:1, 0:P], AX.X, ALU.max, apply_absolute_value=True).then_inc(s_v, 1)
                e.wait_ge(s_v, done + 2)
                e.tensor_scalar(flag[:, :], flag_f[:, 0:1], SAFE_BOUND / DH, None, ALU.is_gt).then_inc(s_v, 1)

            @block.gpsimd
            def _(e):
                e.memset(below[:, :], 1.0).then_inc(s_p, 1)
                e.wait_ge(s_p, 1)
                e.affine_select(out=below[:, :], in_=below[:, :], compare_op=ALU.is_ge, fill=0.0,
                                base=-1, pattern=[[1, P]], channel_multiplier=-1).then_inc(s_p, 1)

            @block.tensor
            def _(e):
                e.wait_ge(s_v, 5)
                e.transpose(R[0:1, 0:P], wq_scale[:, :], k["ident"][:, :]).then_inc(s_t, 1)

        ph = Phase(nc, "a", ctx, 2)
        job_release = []

        def job(fill, after, key, release, stage=1):
            j = len(job_release)
            free = ("prev", job_release_tail[j % 2]) if j < 2 else job_release[j - 2]
            job_release.append(release)
            bank = W[j % 2]
            ph.op("tensor", lambda e, it: fill(e, it, bank), [*after, free], key, stage)
            return bank

        job_release_tail = [("v", 0, 1), ("onorm", 2)]

        row_batch = rows_dram.rearrange("(b c p) d -> b p c d", c=CH, p=P)

        def batch(it, stage):
            return it + 1 - stage

        def load_x():
            ph.dma("sync", [lambda e, it: e.dma_start(xb[:, :, :], x_batch[batch(it, 0)])],
                   [("prev", ("xsum",))], ("x",), 0)

        def norm_x():
            def fn(e, it):
                b = batch(it, 0)
                for c in range(CH):
                    ins = e.tensor_scalar(xn[:, c, :], xb[:, c, :], k["mean"][:, bass.ds(CH * b + c, 1)],
                                          k["rstd"][:, bass.ds(CH * b + c, 1)], ALU.subtract, ALU.mult)
                return ins
            ph.op("vector", fn, [("x",), ("prev", ("xturn", KD - 1)), ("prev", ("xrow",)), ("prev", ("xsum",))], ("xn",), 0)
            ph.dma("sync", [lambda e, it: e.dma_start(row_batch[batch(it, 0)][:, :, 0:D], xn[:, :, :])],
                   [("xn",)], ("xrow",), 0)

        def keep_sum():
            ph.op("gpsimd", lambda e, it: e.tensor_copy(ao[:, :, :], xs[:, :, :]),
                  [("attn",), ("prev", ("xsum",))], ("aosum",), 1)
            ph.op("gpsimd", lambda e, it: e.tensor_tensor(xs[:, :, :], xb[:, :, :], xn[:, :, :], ALU.add),
                  [("xn",), ("aosum",)], ("xsum",), 0)

        def turn_x(d):
            def fn(e, it, bank):
                for c in range(CH):
                    ins = e.transpose(bank[:, c * P:(c + 1) * P], xn[:, c, d * P:(d + 1) * P], k["ident"][:, :])
                return ins
            bank = job(fn, [("xn",)], ("xturn", d), ("xlo", d), 0)
            ph.op("scalar", lambda e, it: e.activation(xT[0][:, d, :], bank[:, :], ACT.Copy),
                  [("xturn", d), ("k", "proj", 1)], ("xhi", d), 0)
            ph.op("vector", lambda e, it: e.tensor_tensor(xT[1][:, d, :], bank[:, :], xT[0][:, d, :].bitcast(F32), ALU.subtract),
                  [("xhi", d)], ("xlo", d), 0)

        PRODUCTS = ((0, 0), (0, 1), (1, 0))

        def ready_x(u):
            return [("prev", ("xlo", KD - 1)) if u else ("xlo", KD - 1)]

        def project(n, u, stage):
            def fn(e, it, bank):
                for i, (d, (pw, px)) in enumerate((d, pr) for d in range(KD) for pr in PRODUCTS):
                    ins = e.matmul(bank[:, :], w[n][pw][:, d, u * P:(u + 1) * P], xT[px][:, d, :],
                                   start=(i == 0), stop=(i == KD * len(PRODUCTS) - 1))
                return ins
            bank = job(fn, ready_x(u), (n, "proj", u), (n, "raw", u), stage)
            ph.op("vector", lambda e, it: e.tensor_copy(raw[n][:, :], bank[:, :]), [(n, "proj", u)], (n, "raw", u), stage)
            ph.op("gpsimd", lambda e, it: e.tensor_tensor(sq[n][:, :], raw[n][:, :], raw[n][:, :], ALU.mult),
                  [(n, "raw", u)], (n, "sq", u), stage)

        def rms(n, u, stage):
            bank = job(lambda e, it, bank: e.matmul(bank[:, :], headsum[:, :], sq[n][:, :], start=True, stop=True),
                       [(n, "sq", u)], (n, "ms", u), (n, "ln", u), stage)
            ph.op("scalar", lambda e, it: e.activation(inv[n][:, :], bank[:, :], ACT.Ln, bias=eps_rms[:, 0:1], scale=1.0 / DH),
                  [(n, "ms", u)], (n, "ln", u), stage)
            ph.op("scalar", lambda e, it: e.activation(inv[n][:, :], inv[n][:, :], ACT.Exp, scale=-0.5),
                  [(n, "ln", u)], (n, "inv", u), stage)

        def parts(n, u, stage):
            weight = wq_scale[:, 0:1] if n == "q" else 1.0
            ph.op("vector", lambda e, it: e.scalar_tensor_tensor(full[n][:, :], raw[n][:, :], weight, inv[n][:, :], ALU.mult, ALU.mult),
                  [(n, "inv", u), ("prev", (n, "lo", 0)) if u else (n, "lo", 1)], (n, "full", u), stage)
            out_before = ("prev", (n, "out", 0)) if u else (n, "out", 1)
            ph.op("vector", lambda e, it: e.tensor_copy(part[n][0][:, :], full[n][:, :]),
                  [(n, "full", u), out_before], (n, "hi", u), stage)
            ph.op("gpsimd", lambda e, it: e.tensor_tensor(part[n][1][:, :], full[n][:, :], part[n][0][:, :].bitcast(F32), ALU.subtract),
                  [(n, "hi", u)], (n, "lo", u), stage)
            i = "qk".index(n)
            ph.dma("sync", [lambda e, it, p=p: e.dma_start(parts_dram[u, i, p], part[n][p][:, :].bitcast(F32)) for p in range(2)],
                   [(n, "lo", u), ("prev", (n, "stack", u))], (n, "out", u), stage)
            order = (0, 0, 1) if n == "q" else (0, 1, 0)
            src = parts_dram[u, i].rearrange("s (h d) n -> s d h n", d=DH)
            last = ("qk_done", u)
            free = ("prev", last) if u == 1 or stage else last
            ph.dma("sync", [lambda e, it, r=r, p=p: e.dma_start(stack[n][u][r * DH:(r + 1) * DH, :, :].bitcast(F32), src[p])
                            for r, p in enumerate(order)],
                   [(n, "out", u), free], (n, "stack", u), stage)

        def project_v(i):
            def fn(e, it, bank):
                for c in range(2):
                    at = (2 * i + c) * P
                    for n, (d, (px, pw)) in enumerate((d, pr) for d in range(KD) for pr in PRODUCTS):
                        ins = e.matmul(bank[:, c * D:(c + 1) * D], xT[px][:, d, at:at + P], w["v"][pw][:, d, :],
                                       start=(n == 0), stop=(n == KD * len(PRODUCTS) - 1))
                return ins
            bank = job(fn, [("xlo", KD - 1)], ("vproj", i), ("v", 0, i), 0)
            seen = bank[:, :].rearrange("p (c d) -> p c d", c=2)
            ph.op("vector", lambda e, it: e.tensor_copy(v_next[:, 2 * i:2 * i + 2, :], seen[:, :, P:D]),
                  [("vproj", i), ("v", 1)], ("vnext", i), 0)
            ph.op("vector", lambda e, it: e.tensor_copy(
                v[0][:, 2 * i:2 * i + 2, :, 0:DH], seen[:, :, 0:P].rearrange("p c (h d) -> p c h d", h=HU)),
                [("vproj", i), ("pv_done", 0)], ("v", 0, i), 0)

        def second_v():
            ph.op("gpsimd", lambda e, it: e.tensor_copy(
                v[1][:, :, :, 0:DH], v_next[:, :, :].rearrange("p c (h d) -> p c h d", h=HU)),
                [("prev", ("vnext", 1)), ("pv_done", 1)], ("v", 1), 1)

        s_g = {n: ctx.enter_context(nc.semaphore(f"g_{n}")) for n in ("mm", "red", "neg", "tp", "sh", "dma")}
        needed = {}

        def shift(u):
            pairs = HU * CH // 2

            def n_of(it):
                return 2 * it + u

            def pe(e, it):
                for i in range(pairs):
                    h, c0 = i // 2, 2 * (i % 2)
                    if i >= 2:
                        e.wait_ge(s_g["red"], pairs * n_of(it) + i - 1)
                    for c in range(2):
                        ins = e.matmul(S[i % 2][:, c, :], stack["q"][u][0:3 * DH, h, (c0 + c) * P:(c0 + c + 1) * P],
                                       stack["k"][u][0:3 * DH, h, :], start=True, stop=True)
                    ins.then_inc(s_g["mm"], 1)
                e.wait_ge(s_g["neg"], n_of(it) + 1)
                e.transpose(S[0][0:HU * CH, 0, 0:P], mx[:, :], k["ident"][:, :]).then_inc(s_g["tp"], 1)
                e.wait_ge(s_g["sh"], 3 * n_of(it) + 3)
                e.wait_ge(s_g["dma"], 64 * n_of(it) + 64)

            def dve(e, it):
                for i in range(pairs):
                    e.wait_ge(s_g["mm"], pairs * n_of(it) + i + 1)
                    e.tensor_reduce(mx[:, 2 * i:2 * i + 2], S[i % 2][:, :, :], AX.X, ALU.max).then_inc(s_g["red"], 1)
                e.wait_ge(s_g["red"], pairs * n_of(it) + pairs)
                e.tensor_scalar(mx[:, :], mx[:, :], -1.0, None, ALU.mult).then_inc(s_g["neg"], 1)
                e.wait_ge(s_g["tp"], n_of(it) + 1)
                e.tensor_copy(shf[:, :], S[0][0:HU * CH, 0, 0:P]).then_inc(s_g["sh"], 1)
                e.wait_ge(s_g["sh"], 3 * n_of(it) + 1)
                e.tensor_copy(sh[0][:, :], shf[:, :]).then_inc(s_g["sh"], 1)
                e.wait_ge(s_g["sh"], 3 * n_of(it) + 2)
                e.tensor_tensor(sh[1][:, :], shf[:, :], sh[0][:, :].bitcast(F32), ALU.subtract).then_inc(s_g["sh"], 1)

            def sp(e, it):
                e.wait_ge(s_g["sh"], 3 * n_of(it) + 3)
                e.nop(nofuse=True)
                for i in range(2):
                    e.dma_start(shift_dram[i], sh[i][:, :].bitcast(F32)).then_inc(s_g["dma"], 16)
                e.wait_ge(s_g["dma"], 64 * n_of(it) + 32)
                e.nop(nofuse=True)
                for i in range(2):
                    r = ROW_SHIFT + i
                    e.dma_start(stack["q"][u][r:r + 1, :, :].bitcast(F32),
                                shift_dram[i].rearrange("(o h c) q -> o h (c q)", o=1, h=HU)).then_inc(s_g["dma"], 16)
                e.wait_ge(s_g["dma"], 64 * n_of(it) + 64)
                e.nop(nofuse=True)

            def only(eng, fn):
                def run(e, it):
                    with e.If(needed[eng] > 0):
                        fn(e, it)
                    return None
                return run
            before = [("q", "stack", u), ("k", "stack", u)]
            if u == 0:
                before = [("prev", x) for x in before]
            exp_before = ("exp", 3, G - 1) if u else ("prev", ("exp", 7, G - 1))
            ph.op("tensor", only("tensor", pe), [*before, exp_before])
            ph.op("vector", only("vector", dve))
            ph.op("sync", only("sync", sp))

        def heads(s, j):
            u, g, half = s // 4, s % 4 // 2, s % 2
            h = G * g + j
            st = [("q", "stack", u), ("k", "stack", u)]
            if u == 0:
                st = [("prev", x) for x in st]
            n = G * s + j
            free = [("exp", (n - 2) // G, (n - 2) % G)] if n >= 2 else [("prev", ("exp", 7, G - 2 + n))]

            def fn(e, it):
                for c in range(2):
                    key = 2 * half + c
                    ins = e.matmul(S[j % 2][:, c, :], stack["k"][u][:, h, key * P:(key + 1) * P],
                                   stack["q"][u][:, h, :], start=True, stop=True)
                return ins
            key = ("qk_done", u) if (s % 4 == 3 and j == G - 1) else ("qk", s, j)
            ph.op("tensor", fn, [*st, *free], key)
            freed = [("pv", s - 2, 1)] if s >= 2 else [("prev", ("pv", 6, 1)) if s == 0 else ("pv_done", 1)]
            freed = [x if x != ("pv", 3, 1) else ("pv_done", 0) for x in freed]
            ph.op("scalar", lambda e, it: e.activation(prob[s % 2][:, j, :, :], S[j % 2][:, :, :], ACT.Exp),
                  [key, *freed], ("exp", s, j))

        def weigh(s, c):
            u, g, half = s // 4, s % 4 // 2, s % 2

            def fn(e, it):
                for j in range(G):
                    ins = e.matmul(pv[VW * j:VW * (j + 1), :], v[u][:, 2 * half + c, G * g + j, :],
                                   prob[s % 2][:, j, c, :], start=(half == 0 and c == 0), stop=(half == 1 and c == 1))
                return ins
            q = s // 2
            stage = 2 if s == 7 else 1
            if s == 7:
                after = [("prev", ("exp", s, G - 1)), ("prev", ("v", 1))]
            else:
                after = [("exp", s, G - 1), ("v", 1) if u else ("prev", ("v", 0, 1))]
            if half == 0 and c == 0:
                after.append(("pvcopy", q - 1) if q else ("pvcopy", 3))
            key = ("pv_done", u) if (s % 4 == 3 and c == 1) else ("pv", s, c)
            ph.op("tensor", fn, after, key, stage)
            if half == 1 and c == 1:
                turned_before = {0: ("prev", ("oturn", 2)), 1: ("oturn", 3), 2: ("oturn", 0), 3: ("prev", ("oturn", 1))}[q]
                ph.op("vector", lambda e, it: e.tensor_copy(oT[q % 2][:, :], pv[:, :]), [key, turned_before], ("pvcopy", q), stage)

        def normalise(q, stage=1):
            def fn(e, it, bank):
                for c in range(CH):
                    ins = e.transpose(bank[:, c * P:(c + 1) * P], oT[q % 2][:, c * P:(c + 1) * P], k["ident"][:, :])
                return ins
            bank = job(fn, [("pvcopy", q)], ("oturn", q), ("onorm", q), stage)
            seen = bank[:, :].rearrange("p (c j w) -> p c j w", c=CH, j=G)
            r = rden[q % 2]
            ph.op("vector", lambda e, it: e.reciprocal(r[:, :, :], seen[:, :, :, DH]), [("oturn", q)], ("rden", q), stage)
            free = [("o2turn", KD - 1)] if q == 0 else []
            ph.op("vector", lambda e, it: e.tensor_tensor(
                o_tok[:, :, G * DH * q:G * DH * (q + 1)].rearrange("p c (j d) -> p c j d", j=G),
                seen[:, :, :, 0:DH], r[:, :, :].unsqueeze(3).broadcast_to([P, CH, G, DH]), ALU.mult),
                [("rden", q), *free], ("onorm", q), stage)

        def turn_o(d):
            def fn(e, it, bank):
                for c in range(CH):
                    ins = e.transpose(bank[:, c * P:(c + 1) * P], o_tok[:, c, d * P:(d + 1) * P], k["ident"][:, :])
                return ins
            bank = job(fn, [("onorm", 3)], ("o2turn", d), ("o2", d), 2)
            ph.op("scalar", lambda e, it: e.activation(oT2[:, d, :], bank[:, :], ACT.Copy),
                  [("o2turn", d), ("prev", ("wo", 1))], ("o2", d), 2)

        def project_o(i):
            def fn(e, it, bank):
                for c in range(2):
                    for d in range(KD):
                        ins = e.matmul(bank[:, c * D:(c + 1) * D], oT2[:, d, (2 * i + c) * P:(2 * i + c + 1) * P],
                                       wo[:, d, :], start=(d == 0), stop=(d == KD - 1))
                return ins
            bank = job(fn, [("o2", KD - 1)], ("wo", i), ("woe", i), 2)
            ph.op("vector", lambda e, it: e.tensor_tensor(
                ao[:, 2 * i:2 * i + 2, :], bank[:, :].rearrange("p (c d) -> p c d", c=2), ao[:, 2 * i:2 * i + 2, :], ALU.add),
                [("wo", i), ("prev", ("aosum",))], ("woe", i), 2)
            if i == 1:
                ph.dma("sync", [lambda e, it: e.dma_start(row_batch[it - 1][:, :, D:2 * D], ao[:, :, :])],
                    [("woe", 0), ("woe", 1)], ("attn",), 2)

        def route(fn, eng="vector", after=(), key=None):
            ph.op(eng, fn, after, key, 1, "route")

        def bits_ask(i):
            before = ("r_z", i - 1) if i else ("r_init",)
            if i == 0:
                route(lambda e, it: e.memset(zcur[:, :], -2 ** 31), after=[("prev", ("r_taken",))], key=("r_init",))
            route(lambda e, it: e.tensor_tensor(zc[:, :], zcur[:, :].broadcast_to([P, CAND]), cand_bits[:, i, :], ALU.bitwise_xor),
                  after=[before], key=("r_zc", i))
            route(lambda e, it: e.tensor_scalar(sgn[:, :], zc[:, :], 31, 1, ALU.arith_shift_right, ALU.logical_shift_right),
                  after=[("r_zc", i)], key=("r_sg", i))
            route(lambda e, it: e.tensor_tensor(thr[:, :], zc[:, :], sgn[:, :], ALU.bitwise_xor),
                  after=[("r_sg", i)], key=("r_th", i))
            route(lambda e, it: e.tensor_tensor(
                ge[:, :, :], k["scores"][:, bass.ds(it, 1), :].broadcast_to([P, CAND, NT]),
                thr[:, :].bitcast(F32).unsqueeze(2).broadcast_to([P, CAND, NT]), ALU.is_ge),
                after=[("r_th", i)], key=("r_ge", i))
            route(lambda e, it: e.tensor_reduce(part_cnt[:, :], ge[:, :, :], AX.X, ALU.add),
                  after=[("r_ge", i)], key=("r_pc", i))

        def bits_answer(i):
            route(lambda e, it: e.matmul(R[:, 0:CAND], ones_h[:, :], part_cnt[:, :], start=True, stop=True),
                  "tensor", [("r_pc", i)], ("r_cnt", i))
            route(lambda e, it: e.tensor_scalar(gem[:, :], R[:, 0:CAND], float(C), None, ALU.is_ge, ALU.add, accum_out=digit[:, :]),
                  after=[("r_cnt", i)], key=("r_dg", i))
            route(lambda e, it: e.tensor_scalar(zadd[:, :], digit[:, :], steps_f[:, i:i + 1], None, ALU.mult),
                  after=[("r_dg", i)], key=("r_za", i))
            route(lambda e, it: e.tensor_tensor(zcur[:, :], zcur[:, :], zadd[:, :].bitcast(I32), ALU.bitwise_xor),
                  after=[("r_za", i)], key=("r_z", i))

        def ranks(src, after, key):
            def fn(e, it):
                e.matmul(R[:, NT:2 * NT], below[:, :], src[:, :], start=True, stop=True)
                return e.matmul(R[:, 2 * NT:3 * NT], ones_h[:, :], src[:, :], start=True, stop=True)
            route(fn, "tensor", after, (key, "mm"))

        def rank_rows(key):
            route(lambda e, it: e.tensor_copy(cols[:, :], R[:, 2 * NT:3 * NT]), after=[(key, "mm")], key=(key, "col"))
            route(lambda e, it: e.tensor_tensor_scan(csum[:, :], cols[:, :], zero[:, :], 0.0, ALU.add, ALU.add),
                  after=[(key, "col")], key=(key, "scan"))
            route(lambda e, it: e.tensor_tensor(csum[:, :], csum[:, :], cols[:, :], ALU.subtract),
                  after=[(key, "scan")], key=(key, "before"))

        def choose():
            last = STEPS - 1
            route(lambda e, it: e.tensor_scalar(sgn[:, 0:1], zcur[:, :], 31, 1, ALU.arith_shift_right, ALU.logical_shift_right),
                  after=[("r_z", last)], key=("c_sg",))
            route(lambda e, it: e.tensor_tensor(thr[:, 0:1], zcur[:, :], sgn[:, 0:1], ALU.bitwise_xor), after=[("c_sg",)], key=("c_th",))

            def flags(dst, op):
                return lambda e, it: e.tensor_tensor(dst[:, :], k["scores"][:, bass.ds(it, 1), :].rearrange("p o t -> p (o t)"),
                                                     thr[:, 0:1].bitcast(F32).broadcast_to([P, NT]), op)
            route(flags(gt, ALU.is_gt), after=[("c_th",)], key=("c_gt",))
            route(flags(eq, ALU.is_equal), key=("c_eq",))
            route(lambda e, it: e.tensor_reduce(gt_cnt[:, :], gt[:, :], AX.X, ALU.add), after=[("c_gt",)], key=("c_gc",))

        def missing():
            route(lambda e, it: e.matmul(R[:, 0:1], ones_h[:, :], gt_cnt[:, :], start=True, stop=True), "tensor", [("c_gc",)], ("c_gn",))
            route(lambda e, it: e.tensor_scalar(need[:, :], R[:, 0:1], -1.0, float(C), ALU.mult, ALU.add), after=[("c_gn",)], key=("c_need",))

        def ties():
            ranks(eq, [("c_eq",), ("c_need",)], "tie")

        def choose_ties():
            rank_rows("tie")
            route(lambda e, it: e.tensor_tensor(rank[:, :], R[:, NT:2 * NT], csum[:, :], ALU.add), after=[("tie", "before")], key=("c_rank",))
            route(lambda e, it: e.scalar_tensor_tensor(tie[:, :], rank[:, :], need[:, 0:1], eq[:, :], ALU.is_lt, ALU.mult),
                  after=[("c_rank",)], key=("c_tie",))
            route(lambda e, it: e.tensor_tensor(sel[:, :], gt[:, :], tie[:, :], ALU.add), after=[("c_tie",)], key=("c_sel",))
            route(lambda e, it: e.tensor_copy(sel_i[:, :], sel[:, :]), after=[("c_sel",)], key=("c_seli",))

        def place():
            rank_rows("slot")
            route(lambda e, it: e.tensor_tensor(rank2[:, :], R[:, NT:2 * NT], csum[:, :], ALU.add), after=[("slot", "before")], key=("p_rank",))
            route(lambda e, it: e.scalar_tensor_tensor(rank2[:, :], rank2[:, :], base[:, 0:1], sel[:, :], ALU.add, ALU.mult),
                  after=[("p_rank",)], key=("p_slot",))
            route(lambda e, it: e.tensor_tensor(slot[:, :], slot[:, :], rank2[:, :], ALU.add), after=[("p_slot",)], key=("p_sum",))
            route(lambda e, it: e.tensor_copy(slot_i[:, :], slot[:, :]), after=[("p_sum",)], key=("p_slots",))
            route(lambda e, it: e.tensor_scalar(base[:, :], base[:, :], float(C), None, ALU.add), key=("p_base",))
            ph.apart.add(("r_taken",))
            route(lambda e, it: e.copy_predicated(
                k["scores"][:, :, :], sel_i[:, :].unsqueeze(1).broadcast_to([P, E, NT]),
                lowest[:, :].unsqueeze(1).broadcast_to([P, E, NT])),
                after=[("p_base",)], key=("r_taken",))

        order_first = E

        def order_tiles():
            def now(e, it):
                e.wait_ge(*ph.value(("p_slots",), E - 1))
                at = bass.ds(ORDERED * (it - order_first), ORDERED)
                e.tensor_copy(slot_now[:, :], slot_i[:, at])
                return e.tensor_copy(token_now[:, :], k["tokens"][:, at])
            ph.op("gpsimd", now, [("prev", ("order", ORDERED - 1))], ("now",), 1, "order")
            ph.first[ph.where[("now",)][0]] = order_first

        def order_tile(t):
            ph.dma("gpsimd", [lambda e, it: e.indirect_dma_start(
                out=order_dram, out_offset=bass.IndirectOffsetOnAxis(ap=slot_now[:, t:t + 1], axis=0),
                in_=token_now[:, t:t + 1], in_offset=None)], [("now",)], ("order", t), 1, "order")
            ph.first[ph.where[("order", t)][0]] = order_first

        def unit(u, stage, at):
            return [(at, lambda: project("q", u, stage)), (at, lambda: project("k", u, stage)),
                    (at + 1, lambda: rms("q", u, stage)), (at + 2, lambda: rms("k", u, stage)),
                    (at + 2, lambda: parts("q", u, stage)), (at + 3, lambda: parts("k", u, stage))]

        work = unit(1, 1, 0) + unit(0, 0, 8) + [
            (0, load_x), (2, second_v), (2, lambda: normalise(3, 2)), (3, lambda: turn_o(0)), (3, lambda: turn_o(1)),
            (4, lambda: project_o(0)), (4, norm_x), (5, lambda: project_o(1)),
            (6, lambda: turn_x(0)), (7, lambda: turn_x(1)),
            (7, lambda: normalise(0)), (11, lambda: normalise(1)), (15, lambda: normalise(2)),
            (12, lambda: project_v(0)), (13, lambda: project_v(1)), (13, keep_sum),
            (0, order_tiles)] + [(2 * t, lambda t=t: order_tile(t)) for t in range(ORDERED)]
        ask = {i: (lambda i=i: bits_ask(i)) for i in range(STEPS)}
        answer = {i: (lambda i=i: bits_answer(i)) for i in range(STEPS)}
        ask[STEPS], answer[STEPS] = choose, missing
        answer[STEPS + 1] = ties
        ask[STEPS + 2] = choose_ties
        answer[STEPS + 2] = lambda: ranks(sel, [("c_sel",)], "slot")
        ask[STEPS + 3] = place

        for s in range(8):
            if s % 4 == 0:
                shift(s // 4)
            for half in range(2):
                point = 2 * s + half
                ask.get(point, lambda: None)()
                heads(s, 2 * half)
                heads(s, 2 * half + 1)
                weigh(s - 1 if s else 7, half)
                for at, fn in work:
                    if at == point:
                        fn()
                answer.get(point, lambda: None)()
        assert len(job_release) % 2 == 0 and job_release[-2:] == job_release_tail, job_release

        with nc.Block() as block:
            def program_for(eng):
                def program(e):
                    if eng in ("tensor", "vector", "sync"):
                        needed[eng] = e.value_load(flag[0:1, 0:1], min_val=0, max_val=1)
                    for its, stages, groups in plan:
                        if isinstance(its, int):
                            ph.body(eng, e, its, stages, groups)
                        else:
                            with e.Fori(its[0], its[1]) as it:
                                ph.body(eng, e, it, stages, groups)
                    if eng == "sync":
                        e.wait_ge(*ph.value(("attn",), B))
                        e.wait_ge(*ph.value(("xrow",), B - 2))
                        for t in range(ORDERED):
                            e.wait_ge(*ph.value(("order", t), B - 1))
                return program
            both, rest = {"", "route"}, {"", "order"}
            plan = [(-1, {0}, both), (0, {0, 1}, both), ((1, E), {0, 1, 2}, both),
                    (E, {0, 1, 2}, rest), ((E + 1, B - 1), {0, 1, 2}, rest), (B - 1, {1, 2}, rest), (B, {2}, rest)]
            for eng in ("sync", "scalar", "vector", "gpsimd", "tensor"):
                on_engine(block, eng)(program_for(eng))


def experts(nc, a, rows_dram, order_dram, out, k):
    U = 2
    UP = 4
    assert C == U * N and NFC % UP == 0
    with ExitStack() as ctx:
        def sb(name, shape, dt=F32):
            return ctx.enter_context(nc.sbuf_tensor(name, shape, dt))

        w1raw = sb("w1raw", [P, KD, F])
        w2raw = sb("w2raw", [P, NFC, D])
        w1 = [sb(f"w1_{i}", [P, KD, F], F32R) for i in range(2)]
        w2 = [sb(f"w2_{i}", [P, NFC, D], F32R) for i in range(2)]
        b1 = sb("b1", [P, E, NFC])
        b2 = sb("b2", [P, E, D])
        b2_now = [sb(f"b2_now{u}", [P, D]) for u in range(U)]
        order = sb("order_s", [P, E, U, CH], I32)
        rows = [sb(f"rows{u}", [P, CH], I32) for u in range(U)]
        rows_in = [sb(f"rows_in{u}", [P, CH], I32) for u in range(U)]
        g = [sb(f"g{u}", [P, CH, 2 * D]) for u in range(U)]
        z = sb("e_z", [P, CH, D])
        nf = sb("nf", [P, KD, N])
        nT = [[sb(f"nT{u}{i}", [P, KD, N], F32R) for i in range(2)] for u in range(U)]
        act = [sb(f"act{i}", [P, N]) for i in range(UP)]
        hid = [sb(f"hid{i}", [P, NFC, N], F32R) for i in range(2)]
        y = [sb(f"y{u}", [P, CH, D]) for u in range(U)]
        stats, aggr, veps, rstd, nmean, shift = (
            sb(f"e_{n}", s) for n, s in (("st", [P, CH, 6]), ("mv", [P, CH, 2]), ("ve", [P, CH]), ("rs", [P, CH]),
                                         ("nm", [P, CH]), ("sh", [P, CH])))
        up = [ctx.enter_context(nc.psum_tensor(f"up{i}", [P, N], F32)) for i in range(UP)]
        turned = [ctx.enter_context(nc.psum_tensor(f"tu{i}", [P, N], F32)) for i in range(KD)]
        down = [ctx.enter_context(nc.psum_tensor(f"dn{i}", [P, N], F32)) for i in range(2)]
        PRODUCTS = ((0, 0), (0, 1), (1, 0))

        s_c = ctx.enter_context(nc.semaphore("e_c"))
        with nc.Block() as block:
            @block.sync
            def _(e):
                loads = [(b1[:, :, :], a["b1"]), (b2[:, :, :].rearrange("p e d -> p (e d)"),
                          a["b2"].rearrange("(o e) d -> o (e d)", o=1).broadcast_to([P, E * D])),
                         (order[:, :, :, :].rearrange("p e u c -> p (e u c)"), order_dram.rearrange("(t p) o -> p (t o)", p=P))]
                for dst, src in loads:
                    e.dma_start(dst, src, allow_slow_non_contiguous=True).then_inc(s_c, 16)
                e.wait_ge(s_c, 16 * len(loads))

        ph = Phase(nc, "e", ctx, 1)

        def ex(it, stage):
            return it + 1 - stage

        def load_weights(name, raw, src):
            last = ("prev", (name, "lo", NFC - 1 if name == "w2" else KD - 1))
            ph.dma("sync", [lambda e, it: e.dma_start(raw[:, :, :], src[ex(it, 0)])], [last], (name, "raw"), 0)

        def split(name, raw, parts, last_use):
            n = raw.shape[1]
            step = n // KD
            for i in range(0, n, step):
                at = slice(i, i + step)
                ph.op("scalar", lambda e, it, at=at: e.activation(parts[0][:, at, :], raw[:, at, :], ACT.Copy),
                      [(name, "raw"), last_use], (name, "hi", i + step - 1), 0)
                ph.op("vector", lambda e, it, at=at: e.tensor_tensor(
                    parts[1][:, at, :], raw[:, at, :], parts[0][:, at, :].bitcast(F32), ALU.subtract),
                    [(name, "hi", i + step - 1)], (name, "lo", i + step - 1), 0)

        def next_rows(u):
            def fn(e, it):
                return e.tensor_copy(rows[u][:, :], rows_in[u][:, :])
            ph.op("gpsimd", fn, [("prev", ("gather", u, CH - 1)), *[("prev", ("scatter", u, c)) for c in range(CH)]], ("rows", u), 1)
            ph.op("gpsimd", lambda e, it: e.tensor_copy(rows_in[u][:, :], order[:, bass.ds(ex(it, 0), 1), u, :].rearrange("p o c -> p (o c)")),
                  [("rows", u), *[("prev", ("gather", u, c)) for c in range(CH)]], ("rows_in", u), 0)

        def gather(u, c):
            ph.dma("gpsimd", [lambda e, it: e.indirect_dma_start(
                out=g[u][:, c, :], out_offset=None, in_=rows_dram,
                in_offset=bass.IndirectOffsetOnAxis(ap=rows_in[u][:, c:c + 1], axis=0))],
                [("rows_in", u), ("y", u, c)], ("gather", u, c), 0)

        def other(u, *step):
            return ("prev", step) if u else step

        def gathered(u, c):
            return ("prev", ("gather", u, c)) if u else ("gather", u, c)

        def prepare(u):
            stage = u
            pieces = {}

            def stat(c):
                ph.op("vector", lambda e, it: e.bn_stats(stats[:, c, :], g[u][:, c, 0:D]),
                      [gathered(u, c), other(u, "aggr", 1 - u)], ("stat", u, c), stage)

            def aggregate():
                def fn(e, it):
                    for c in range(CH):
                        ins = e.bn_aggr(aggr[:, c, :], stats[:, c, :])
                    return ins
                ph.apart.add(("aggr", u))
                ph.op("vector", fn, [("stat", u, CH - 1), other(u, "shift", 1 - u)], ("aggr", u), stage)
                ph.op("gpsimd", lambda e, it: e.tensor_tensor(veps[:, :], aggr[:, :, 1], k["eps_ln"][:, :], ALU.add),
                      [("aggr", u)], ("veps", u), stage)
                ph.op("gpsimd", lambda e, it: e.tensor_tensor(nmean[:, :], aggr[:, :, 0], k["minus"][:, :], ALU.mult),
                      [other(u, "shift", 1 - u)], ("nmean", u), stage)
                ph.op("gpsimd", lambda e, it: e.tensor_tensor(rstd[:, :], veps[:, :], k["half"][:, :], ALU.pow),
                      [("veps", u), other(u, "scale", 1 - u)], ("rstd", u), stage)
                ph.op("gpsimd", lambda e, it: e.tensor_tensor(shift[:, :], nmean[:, :], rstd[:, :], ALU.mult),
                      [("rstd", u)], ("shift", u), stage)

            def scale():
                def fn(e, it):
                    for c in range(CH):
                        ins = e.activation(z[:, c, :], g[u][:, c, 0:D], ACT.Identity, bias=shift[:, c:c + 1], scale=rstd[:, c:c + 1])
                    return ins
                ph.op("scalar", fn, [("shift", u), other(u, "turn", 1 - u, KD - 1)], ("scale", u), stage)

            def add_bias():
                def now(e, it):
                    return e.tensor_copy(b2_now[u][:, :], b2[:, bass.ds(ex(it, stage), 1), :].rearrange("p o d -> p (o d)"))
                ph.op("gpsimd", now, [("prev", ("bias", u))], ("b2", u), stage)
                ph.op("gpsimd", lambda e, it: e.tensor_tensor(
                    g[u][:, :, D:2 * D], g[u][:, :, D:2 * D], b2_now[u][:, :].unsqueeze(1).broadcast_to([P, CH, D]), ALU.add),
                    [("b2", u), gathered(u, CH - 1)], ("bias", u), stage)

            def turn(d):
                def fn(e, it):
                    for c in range(CH):
                        ins = e.transpose(turned[d][:, c * P:(c + 1) * P], z[:, c, d * P:(d + 1) * P], k["ident"][:, :])
                    return ins
                ph.op("tensor", fn, [("scale", u), other(u, "affine", 1 - u, d)], ("turn", u, d), stage)
                ph.op("scalar", lambda e, it: e.activation(nf[:, d, :], turned[d][:, :], ACT.Identity,
                                                           bias=k["offset"][:, d:d + 1], scale=k["gain"][:, d:d + 1]),
                      [("turn", u, d), other(u, "nlo", 1 - u, d)], ("affine", u, d), stage)
                ph.op("vector", lambda e, it: e.tensor_copy(nT[u][0][:, d, :], nf[:, d, :]),
                      [("affine", u, d), ("up", u, NFC - 1) if u == 0 else ("prev", ("up", u, NFC - 1))], ("nhi", u, d), stage)
                ph.op("vector", lambda e, it: e.tensor_tensor(nT[u][1][:, d, :], nf[:, d, :], nT[u][0][:, d, :].bitcast(F32), ALU.subtract),
                      [("nhi", u, d)], ("nlo", u, d), stage)

            for c in range(CH):
                pieces["stat", c] = lambda c=c: stat(c)
            pieces["aggregate"], pieces["scale"], pieces["bias"] = aggregate, scale, add_bias
            for d in range(KD):
                pieces["turn", d] = lambda d=d: turn(d)
            return pieces

        def layer_up(u, fc):
            def before(name, back):
                i = (NFC * u + fc) - back
                step = (name, i // NFC % 2, i % NFC)
                return ("prev", step) if i < 0 else step
            bank, held = up[fc % UP], act[fc % UP]

            def fn(e, it):
                for i, (d, (pw, px)) in enumerate((d, pr) for d in range(KD) for pr in PRODUCTS):
                    ins = e.matmul(bank[:, :], w1[pw][:, d, fc * P:(fc + 1) * P], nT[u][px][:, d, :],
                                   start=(i == 0), stop=(i == KD * len(PRODUCTS) - 1))
                return ins
            ready = ("nlo", u, KD - 1) if u else ("prev", ("nlo", u, KD - 1))
            ph.op("tensor", fn, [("prev", ("w1", "lo", KD - 1)), ready, before("gelu", UP)], ("up", u, fc))
            ph.apart.add(("gelu", u, fc))
            ph.op("scalar", lambda e, it: e.activation(held[:, :], bank[:, :], ACT.Gelu_apprx_tanh,
                                                       bias=b1[:, bass.ds(it, 1), fc:fc + 1].rearrange("p o c -> p (o c)")),
                  [("up", u, fc), before("hlo", UP)], ("gelu", u, fc))
            free = ("down", 0, CH - 1) if u else ("prev", ("down", 1, CH - 1))
            if fc % 2:
                ph.op("scalar", lambda e, it: e.activation(hid[0][:, fc, :], held[:, :], ACT.Copy),
                      [("gelu", u, fc), free], ("hhi", u, fc))
            else:
                ph.op("vector", lambda e, it: e.tensor_copy(hid[0][:, fc, :], held[:, :]),
                      [("gelu", u, fc), free], ("hhi", u, fc))
            ph.op("vector", lambda e, it: e.tensor_tensor(hid[1][:, fc, :], held[:, :], hid[0][:, fc, :].bitcast(F32), ALU.subtract),
                  [("hhi", u, fc)], ("hlo", u, fc))

        def layer_down(u, c):
            bank = down[c % 2]
            for fc in range(NFC):
                def fn(e, it, fc=fc):
                    for i, (ph_, pw) in enumerate(PRODUCTS):
                        ins = e.matmul(bank[:, 0:D], hid[ph_][:, fc, c * P:(c + 1) * P], w2[pw][:, fc, :],
                                       start=(fc == 0 and i == 0), stop=(fc == NFC - 1 and i == len(PRODUCTS) - 1))
                    return ins
                after = []
                if fc == 0:
                    bank_before = ("y", u, c - 2) if c >= 2 else ("y", 0, c + 2) if u else ("prev", ("y", 1, c + 2))
                    after = [("prev", ("w2", "lo", NFC - 1)), bank_before]
                if c == 0:
                    after.append(("hlo", u, fc))
                ph.op("tensor", fn, after, ("down", u, c) if fc == NFC - 1 else None)
            biased = ("bias", u) if u else ("prev", ("bias", u))
            ph.op("vector", lambda e, it: e.tensor_tensor(y[u][:, c, :], down[c % 2][:, 0:D], g[u][:, c, D:2 * D], ALU.add),
                  [("down", u, c), biased, ("prev", ("scatter", u, c))], ("y", u, c))
            ph.dma("gpsimd", [lambda e, it: e.indirect_dma_start(
                out=out, out_offset=bass.IndirectOffsetOnAxis(ap=rows[u][:, c:c + 1], axis=0),
                in_=y[u][:, c, :], in_offset=None)], [("y", u, c), ("rows", u)], ("scatter", u, c))
            gather(u, c)

        load_weights("w1", w1raw, a["w1"])
        load_weights("w2", w2raw, a["w2"])
        for u in range(U):
            pieces = prepare(1 - u)
            next_rows(u)
            for fc in range(NFC):
                layer_up(u, fc)
                if 1 <= fc <= CH:
                    pieces["stat", fc - 1]()
                if fc == CH:
                    pieces["aggregate"]()
                if fc == CH + 2:
                    pieces["scale"]()
                    pieces["bias"]()
            if u == 1:
                split("w1", w1raw, w1, ("up", 1, NFC - 1))
            for c in range(CH):
                layer_down(u, c)
                if c == 0:
                    pieces["turn", 0]()
                    pieces["turn", 1]()
        split("w2", w2raw, w2, ("down", 1, CH - 1))
        run_phase(nc, ph, ["sync", "gpsimd", "vector", "scalar", "tensor"],
                  [(-1, {0}, {""}), (0, {0, 1}, {""}), ((1, E - 1), {0, 1}, {""}), (E - 1, {1}, {""})])
        with nc.Block() as block:
            @block.sync
            def _(e):
                for u in range(U):
                    for c in range(CH):
                        e.wait_ge(*ph.value(("scatter", u, c), E - 1))


def kernel(**inputs):
    import concourse.bacc as bacc
    from concourse.bass_utils import run_bass_kernel_spmd

    def on_partitions(w):
        return w.reshape(-1, P, w.shape[-1]).transpose(1, 0, 2)

    i = {n: np.asarray(v) for n, v in inputs.items()}
    row, col = np.arange(P)[:, None], np.arange(P)[None, :]
    shifts = [BITS * s for s in range(STEPS)][::-1]
    beyond = 0xff7fffff
    cand = np.array([[(c + 1) << s if (c + 1) << s < 2 ** 32 else beyond for c in range(CAND)] for s in shifts],
                    np.uint32).view(np.int32)
    arrays = {
        "x": i["L0_attn_x"],
        "wq": on_partitions(i["L0_attn_Wq"].T), "wk": on_partitions(i["L0_attn_Wk"].T),
        "wv": on_partitions(i["L0_attn_Wv"].T), "wo": on_partitions(i["L0_attn_Wo"].T),
        "qk_w": np.stack([np.tile(i["L0_attn_qn_w"], HU), np.tile(i["L0_attn_kn_w"], HU)], 1),
        "centroids": on_partitions(i["L0_ffn_centroids"].T),
        "ln_g": i["L0_ffn_ln_g"].reshape(KD, P).T, "ln_b": i["L0_ffn_ln_b"].reshape(KD, P).T,
        "w1": i["L0_ffn_w1"].reshape(E, KD, P, F).transpose(0, 2, 1, 3),
        "w2": i["L0_ffn_w2"].reshape(E, NFC, P, D).transpose(0, 2, 1, 3),
        "b1": i["L0_ffn_b1"].reshape(E, NFC, P).transpose(2, 0, 1),
        "b2": i["L0_ffn_b2"],
        "ident": np.eye(P, dtype=np.float32),
        "headsum": (row // DH == col // DH).astype(np.float32),
        "tokens": (np.arange(NT)[None, :] * P + np.arange(P)[:, None]).astype(np.int32),
        "cand_bits": np.broadcast_to(cand[None], (P, STEPS, CAND)),
        "steps_f": np.broadcast_to(np.array([2.0 ** s for s in shifts], np.float32)[None], (P, STEPS)),
    }
    nc = bacc.Bacc("TRN2", target_bir_lowering=False, num_devices=1)
    maps, aps = {}, {}
    for name, v in arrays.items():
        v = np.ascontiguousarray(v)
        maps[f"in_{name}"] = v
        aps[name] = nc.dram_tensor(f"in_{name}", v.shape, mybir.dt.from_np(v.dtype), kind="ExternalInput").ap()
    out = nc.dram_tensor("out", (T, D), F32, kind="ExternalOutput").ap()
    build(nc, aps, out)
    r = run_bass_kernel_spmd(nc, [maps], core_ids=[0])
    return r.results[0]["out"].reshape(B, N, D)
```

```python
import numpy as np
import concourse.bass as bass
from concourse import mybir
from contextlib import ExitStack

F32 = mybir.dt.float32
F32R = mybir.dt.float32r
BF16 = mybir.dt.bfloat16
I32 = mybir.dt.int32
U32 = mybir.dt.uint32
ALU = mybir.AluOpType
ACT = mybir.ActivationFunctionType
AX = mybir.AxisListType

B, N, D = 16, 512, 256
H, DH = 16, 16
E, F = 8, 1024
T = B * N
C = T // E
P = 128
NT = T // P
CH = N // P
KD = D // P
HU = P // DH
NFC = F // P
LN_EPS = 1e-5
RMS_EPS = float(np.finfo(np.float32).eps)
SCALE = DH ** -0.5
ROW_SHIFT, ROWS = 64, 96
SAFE_BOUND = 60.0
BITS = 3
STEPS = -(-32 // BITS)
CAND = 2 ** BITS - 1


class Phase:

    def __init__(self, nc, name, ctx, groups=None):
        self.nc, self.name, self.ctx, self.groups = nc, name, ctx, groups or {}
        self.queue, self.where, self.sems, self.per = {}, {}, {}, {}
        self.first = {}
        self.owed = {}
        self.apart = set()

    def sem(self, name):
        if name not in self.sems:
            self.sems[name] = self.ctx.enter_context(self.nc.semaphore(f"{self.name}_{name}"))
            self.per[name] = 0
        return name

    def op(self, eng, fn, after=(), key=None, stage=1, group=""):
        if key is not None:
            s = self.sem(f"{eng}{group}")
            self.per[s] += 1
            assert key not in self.where, key
            self.where[key] = (s, self.per[s])
            if group:
                self.first[s] = self.groups[group] - 1
                self.owed.setdefault(eng, set()).add(s)
        self.queue.setdefault(eng, []).append((fn, tuple(after), key, stage, group, 1))

    def dma(self, eng, fns, after=(), key=None, stage=1, group=""):
        s = self.sem("dma_" + "_".join(map(str, key)) if isinstance(key, tuple) else f"dma_{key}")
        self.per[s] += 16 * len(fns)
        self.where[key] = (s, self.per[s])
        if eng == "gpsimd":
            self.first[s] = self.groups[group] if group else stage - 1
        elif group:
            self.first[s] = self.groups[group] - 1
            self.owed.setdefault(eng, set()).add(s)

        def issue(e, it):
            for f in fns:
                f(e, it).then_inc(self.sems[s], 16)
            return None
        self.queue.setdefault(eng, []).append((issue, tuple(after), key, stage, group, 16 * len(fns)))

    def credit(self, eng, e):
        for s in sorted(self.owed.get(eng, ())):
            e.sem_inc(self.sems[s], self.per[s])

    def value(self, step, it):
        s, k = self.where[step]
        return self.sems[s], (it - self.first.get(s, -1)) * self.per[s] + k

    def wait(self, e, after, it, apart):
        for a in after:
            back = 0
            if a[0] == "prev":
                back, a = 1, a[1]
            if back and isinstance(it, int) and self.value(a, it - back)[1] <= 0:
                continue
            e.wait_ge(*self.value(a, it - back))
            if apart and not isinstance(it, int):
                e.nop(nofuse=True)

    def body(self, eng, e, it, stages, groups):
        skipped = {}
        waited = {}

        def settle():
            for s, n in skipped.items():
                e.drain()
                e.sem_inc(self.sems[s], n)
            skipped.clear()

        for fn, after, key, stage, group, n in self.queue.get(eng, []):
            if stage not in stages or group not in groups:
                name = self.where[key][0] if key else ""
                over = not key or name in self.first or (name.startswith("dma_") and stage < min(stages))
                if not over and group in groups:
                    s = self.where[key][0]
                    skipped[s] = skipped.get(s, 0) + n
                continue
            settle()
            need = []
            for a in after:
                back, b = (1, a[1]) if a[0] == "prev" else (0, a)
                if b not in self.where:
                    raise KeyError(b)
                s, k = self.where[b]
                if waited.get(s, (-9, 0)) < (-back, k):
                    waited[s] = (-back, k)
                    need.append(a)
            self.wait(e, need, it, eng in ("gpsimd", "sync") or key in self.apart)
            ins = fn(e, it)
            if key is not None and ins is not None:
                ins.then_inc(self.sems[self.where[key][0]], 1)
        settle()


def on_engine(block, eng):
    return {"sync": block.sync, "scalar": block.scalar, "vector": block.vector,
            "gpsimd": block.gpsimd, "tensor": block.tensor}[eng]


def run_phase(nc, phase, engines, plan, before):
    with nc.Block() as block:
        for eng in engines:
            def program(e, eng=eng):
                if eng in before:
                    before[eng](e)
                for its, stages, groups in plan:
                    if isinstance(its, int):
                        phase.body(eng, e, its, stages, groups)
                    elif any(x[3] in stages and x[4] in groups for x in phase.queue.get(eng, [])):
                        with e.Fori(its[0], its[1]) as it:
                            phase.body(eng, e, it, stages, groups)
            on_engine(block, eng)(program)


def build(nc, a, out):
    x_batch = a["x"].rearrange("b (c p) d -> b p c d", p=P)
    rows_dram = nc.dram_tensor("rows", (T, 2 * D), F32, kind="Internal").ap()
    order_dram = nc.dram_tensor("order", (T, 1), I32, kind="Internal").ap()
    parts_dram = nc.dram_tensor("parts", (2, 2, 2, P, N), F32, kind="Internal").ap()
    shift_dram = nc.dram_tensor("shifts", (2, HU * CH, P), F32, kind="Internal").ap()

    with ExitStack() as top:
        def sb(name, shape, dt, ctx=top):
            return ctx.enter_context(nc.sbuf_tensor(name, shape, dt))

        k = {}
        k["ident"] = sb("ident", [P, P], F32)
        k["gain"] = sb("gain", [P, KD], F32)
        k["offset"] = sb("offset", [P, KD], F32)
        k["eps_ln"] = sb("eps_ln", [P, CH], F32)
        k["half"] = sb("half", [P, CH], F32)
        k["minus"] = sb("minus", [P, CH], F32)
        k["order"] = sb("order_rows", [P, E, C // N, CH], I32)
        k["tokens"] = sb("tokens", [P, NT], I32)
        attention_and_routing(nc, a, x_batch, rows_dram, order_dram, parts_dram, shift_dram, k)
        experts(nc, a, rows_dram, out, k)


class LayerNorm:

    def __init__(self, ph, tag, src, tiles, k, dst, stage, group=""):
        self.ph, self.tag, self.src, self.k, self.dst = ph, tag, src, k, dst
        self.stage, self.group = stage, group
        self.stats, self.aggr, self.veps, self.rstd = tiles

    def moments(self, after, free_aggr=()):
        ph, tag, k, at = self.ph, self.tag, self.k, (self.stage, self.group)

        def stat(e, it):
            for c in range(CH):
                ins = e.bn_stats(self.stats[:, c, :], self.src[:, c, :])
            return ins
        ph.op("vector", stat, after, (tag, "stat"), *at)

        def agg(e, it):
            for c in range(CH):
                ins = e.bn_aggr(self.aggr[:, c, :], self.stats[:, c, :])
            return ins
        ph.apart.add((tag, "agg"))
        ph.op("vector", agg, [(tag, "stat"), *free_aggr], (tag, "agg"), *at)
        ph.op("gpsimd", lambda e, it: e.tensor_tensor(self.veps[:, :], self.aggr[:, :, 1], k["eps_ln"][:, :], ALU.add),
              [(tag, "agg")], (tag, "veps"), *at)
        ph.op("gpsimd", lambda e, it: e.tensor_tensor(self.rstd[:, :], self.veps[:, :], k["half"][:, :], ALU.pow),
              [(tag, "veps")], (tag, "rstd"), *at)

    def scale(self, free_dst=()):
        def fn(e, it):
            for c in range(CH):
                ins = e.tensor_scalar(self.dst[:, c, :], self.src[:, c, :], self.aggr[:, c, 0:1],
                                      self.rstd[:, c:c + 1], ALU.subtract, ALU.mult)
            return ins
        self.ph.op("vector", fn, [(self.tag, "rstd"), *free_dst], (self.tag, "out"), self.stage, self.group)


def norm_tiles(sb, name):
    return [sb(f"{name}_{n}", s, F32) for n, s in (("st", [P, CH, 6]), ("mv", [P, CH, 2]), ("ve", [P, CH]), ("rs", [P, CH]))]


def attention_and_routing(nc, a, x_batch, rows_dram, order_dram, parts_dram, shift_dram, k):
    G = 4
    VW = 32
    SCORED = 4
    FIRST = {"score": 0, "route": B // SCORED, "order": B // SCORED + E}
    ORDERED = NT // (B - FIRST["order"])
    with ExitStack() as ctx:
        def sb(name, shape, dt):
            return ctx.enter_context(nc.sbuf_tensor(name, shape, dt))

        def ps(name, shape):
            return ctx.enter_context(nc.psum_tensor(name, shape, F32))

        ctx.enter_context(nc.allow_low_precision(reason="counts of at most NT tokens are exact in bfloat16"))
        w = {n: [sb(f"w{n}{i}", [P, KD, D], F32R) for i in range(2)] for n in "qkv"}
        wo = sb("wo", [P, KD, D], F32)
        headsum = sb("headsum", [P, P], F32)
        ones_h = sb("ones_h", [P, P], BF16)
        below = sb("below", [P, P], BF16)
        qk_w = sb("qk_w", [P, 2], F32)
        wq_scale = sb("wq_scale", [P, 1], F32)
        eps_rms = sb("eps_rms", [P, 1], F32)
        flag_f = sb("flag_f", [1, 2], F32)
        flag = sb("flag", [1, 1], I32)
        xb = sb("xb", [P, CH, D], F32)
        xn = sb("xn", [P, CH, D], F32)
        xT = [sb(f"xT{i}", [P, KD, N], F32R) for i in range(2)]
        raw = {n: sb(f"raw{n}", [P, N], F32) for n in "qk"}
        work_qk = {n: sb(f"work{n}", [P, N], F32) for n in "qk"}
        part = {n: [sb(f"part{n}{i}", [P, N], F32R) for i in range(2)] for n in "qk"}
        stack = {n: [sb(f"stack{n}{u}", [ROWS, HU, N], F32R) for u in range(2)] for n in "qk"}
        v = [sb(f"v{u}", [P, CH, HU, VW], F32) for u in range(2)]
        v_next = sb("v_next", [P, CH, P], F32)
        prob = [sb(f"prob{i}", [P, G, 2, N], F32) for i in range(2)]
        oT = [sb(f"oT{i}", [P, N], F32) for i in range(2)]
        rden = [sb(f"rden{i}", [P, CH, G], F32) for i in range(2)]
        o_tok = sb("o_tok", [P, CH, D], F32)
        oT2 = sb("oT2", [P, KD, N], F32)
        xs = sb("xs", [P, CH, D], F32)
        ao = sb("ao", [P, CH, D], F32)
        mx = sb("mx", [P, HU * CH], F32)
        sh = [sb(f"sh{i}", [HU * CH, P], F32R) for i in range(2)]
        shf = sb("shf", [HU * CH, P], F32)
        cand_bits = sb("cand_bits", [P, STEPS, CAND], I32)
        steps_f = sb("steps_f", [P, STEPS], F32)
        zc = sb("zc", [P, CAND], I32)
        sgn = sb("sgn", [P, CAND], I32)
        thr = sb("thr", [P, CAND], I32)
        zcur = sb("zcur", [P, 1], I32)
        mask = sb("mask", [P, 1], I32)
        best = sb("best", [P, 1], I32)
        zadd = sb("zadd", [P, 1], U32)
        digit = sb("digit", [P, 1], F32)
        ge = sb("ge", [P, CAND, NT], BF16)
        part_cnt = sb("part_cnt", [P, CAND], BF16)
        gem = sb("gem", [P, CAND], F32)
        gt = sb("gt", [P, NT], BF16)
        gt_cnt = sb("gt_cnt", [P, 1], BF16)
        eq = sb("eq", [P, NT], BF16)
        need = sb("need", [P, 1], F32)
        cols = sb("cols", [P, NT], F32)
        zero = sb("zero", [P, NT], F32)
        csum = sb("csum", [P, NT], F32)
        rank = sb("rank", [P, NT], F32)
        tie = sb("tie", [P, NT], F32)
        sel = sb("sel", [P, NT], BF16)
        sel_i = sb("sel_i", [P, NT], I32)
        rank2 = sb("rank2", [P, NT], F32)
        slot = sb("slot", [P, NT], F32)
        slot_now, place_p, place_t, placed = (sb(n, [P, ORDERED], I32) for n in ("slot_now", "place_p", "place_t", "placed"))
        token_now = sb("token_now", [P, ORDERED], I32)
        base = sb("base", [P, 1], F32)
        lowest = sb("lowest", [P, 1], F32)
        one = sb("one", [P, 1], F32)
        scores = sb("scores", [P, E, NT], F32)
        cent = sb("cent", [P, KD, E], F32)
        feat = [sb(f"feat{i}", [P, CH, D], F32) for i in range(3)]
        featT = sb("featT", [P, KD, N], F32)
        tiles_x = norm_tiles(sb, "nx")
        tiles_feat = [[norm_tiles(sb, f"nf{i}{j}") for j in range(2)] for i in range(2)]

        S = [ps(f"S{i}", [P, 2, N]) for i in range(2)]
        pv = ps("pv", [P, N])
        W = [ps(f"W{i}", [P, N]) for i in range(2)]
        R = ps("R", [P, N])

        s_w, s_hi, s_lo, s_c, s_v, s_t, s_p = (
            ctx.enter_context(nc.semaphore(f"a_{n}")) for n in ("w", "hi", "lo", "c", "v", "t", "p"))
        land = dict(zip("qkv", (o_tok, xs, ao)))
        s_k, s_order = (ctx.enter_context(nc.semaphore(n)) for n in ("a_k", "a_order"))
        LOADS = 8

        def all_set(e):
            e.wait_ge(s_c, 16 * LOADS)
            e.wait_ge(s_hi, 4)
            e.wait_ge(s_lo, 4)
            e.wait_ge(s_v, 3)
            e.wait_ge(s_p, 3)

        def setup_sync(e):
            for n in "qkv":
                e.dma_start(land[n][:, 0:KD, :], a[f"w{n}"]).then_inc(s_w, 16)
            for dst, src in ((qk_w[:, :], a["qk_w"]), (k["ident"][:, :], a["ident"])):
                e.dma_start(dst, src).then_inc(s_k, 16)
            loads = [(headsum[:, :], a["headsum"]),
                     (k["gain"][:, :], a["ln_g"]), (k["offset"][:, :], a["ln_b"]), (cent[:, :, :], a["centroids"]),
                     (wo[:, :, :], a["wo"]), (k["tokens"][:, :], a["tokens"]),
                     (cand_bits[:, :, :], a["cand_bits"]), (steps_f[:, :], a["steps_f"])]
            for dst, src in loads:
                e.dma_start(dst, src).then_inc(s_c, 16)
            assert len(loads) == LOADS
            e.wait_ge(s_v, 3)

        def setup_scalar(e):
            e.preload_act_table_set("natural_log_exp_and_others")
            e.wait_ge(s_w, 16 * 3)
            for n in "qkv":
                e.activation(w[n][0][:, :, :], land[n][:, 0:KD, :], ACT.Copy).then_inc(s_hi, 1)
            e.wait_ge(s_p, 1)
            e.activation(stack["k"][1][:, :, :].rearrange("p h n -> p (h n)"), one[0:ROWS, 0:1].broadcast_to([ROWS, HU * N]),
                         ACT.Copy).then_inc(s_hi, 1)
            all_set(e)

        def setup_vector(e):
            e.wait_ge(s_k, 32)
            e.scalar_tensor_tensor(wq_scale[:, :], qk_w[:, 0:1], SCALE, qk_w[:, 1:2], ALU.mult, ALU.mult).then_inc(s_v, 1)
            e.wait_ge(s_t, 1)
            e.tensor_reduce(flag_f[:, 0:1], R[0:1, 0:P], AX.X, ALU.max, apply_absolute_value=True).then_inc(s_v, 1)
            e.wait_ge(s_v, 2)
            e.tensor_scalar(flag[:, :], flag_f[:, 0:1], SAFE_BOUND / DH, None, ALU.is_gt).then_inc(s_v, 1)
            for i, n in enumerate("qkv"):
                e.wait_ge(s_hi, i + 1)
                e.tensor_tensor(w[n][1][:, :, :], land[n][:, 0:KD, :], w[n][0][:, :, :].bitcast(F32), ALU.subtract).then_inc(s_lo, 1)
            for t, val in ((eps_rms, RMS_EPS), (lowest, float(np.finfo(np.float32).min)), (base, 0.0), (slot, 0.0),
                           (zero, 0.0), (ones_h, 1.0)):
                e.memset(t[:, :], val)
            e.memset(stack["q"][0][:, :, :].bitcast(F32), 0.0).then_inc(s_lo, 1)
            all_set(e)

        def setup_gpsimd(e):
            e.memset(k["eps_ln"][:, :], LN_EPS)
            e.memset(k["minus"][:, :], -1.0)
            e.memset(k["half"][:, :], -0.5)
            e.memset(one[:, :], 1.0)
            e.memset(below[:, :], 1.0).then_inc(s_p, 1)
            e.wait_ge(s_p, 1)
            e.affine_select(out=below[:, :], in_=below[:, :], compare_op=ALU.is_ge, fill=0.0,
                            base=-1, pattern=[[1, P]], channel_multiplier=-1).then_inc(s_p, 1)
            for u in range(2):
                e.memset(v[u][:, :, :, :], 1.0)
            e.memset(stack["k"][0][:, :, :].bitcast(F32), 1.0)
            e.memset(stack["q"][1][:, :, :].bitcast(F32), 0.0).then_inc(s_p, 1)
            all_set(e)

        def setup_tensor(e):
            e.wait_ge(s_v, 1)
            e.wait_ge(s_k, 32)
            e.transpose(R[0:1, 0:P], wq_scale[:, :], k["ident"][:, :]).then_inc(s_t, 1)
            all_set(e)

        ph = Phase(nc, "a", ctx, FIRST)
        job_release = []

        def job(fill, after, key, release, stage=1):
            j = len(job_release)
            free = ("prev", job_release_tail[j % 2]) if j < 2 else job_release[j - 2]
            job_release.append(release)
            bank = W[j % 2]
            ph.op("tensor", lambda e, it: fill(e, it, bank), [*after, free], key, stage)
            return bank

        job_release_tail = [("v", 0, 1), ("onorm", 2)]

        row_batch = rows_dram.rearrange("(b c p) d -> b p c d", c=CH, p=P)

        def batch(it, stage):
            return it + 1 - stage

        def load_x():
            ph.dma("sync", [lambda e, it: e.dma_start(xb[:, :, :], x_batch[batch(it, 0)])],
                   [("prev", ("xsum",))], ("xload",), 0)

        norm = LayerNorm(ph, "x", xb, tiles_x, k, xn, 0)

        def norm_x():
            norm.scale([("prev", ("xturn", KD - 1)), ("prev", ("xrow",)), ("prev", ("xsum",))])
            ph.dma("sync", [lambda e, it: e.dma_start(row_batch[batch(it, 0)][:, :, 0:D], xn[:, :, :])],
                   [("x", "out")], ("xrow",), 0)

        def keep_sum():
            ph.op("vector", lambda e, it: e.tensor_copy(ao[:, :, :], xs[:, :, :]),
                  [("attn",), ("prev", ("xsum",))], ("aosum",), 1)
            ph.op("gpsimd", lambda e, it: e.tensor_tensor(xs[:, :, :], xb[:, :, :], xn[:, :, :], ALU.add),
                  [("x", "out"), ("aosum",)], ("xsum",), 0)

        def turn_x(d):
            def fn(e, it, bank):
                for c in range(CH):
                    ins = e.transpose(bank[:, c * P:(c + 1) * P], xn[:, c, d * P:(d + 1) * P], k["ident"][:, :])
                return ins
            bank = job(fn, [("x", "out")], ("xturn", d), ("xlo", d), 0)
            ph.op("scalar", lambda e, it: e.activation(xT[0][:, d, :], bank[:, :], ACT.Copy),
                  [("xturn", d), ("k", "proj", 1)], ("xhi", d), 0)
            ph.op("vector", lambda e, it: e.tensor_tensor(xT[1][:, d, :], bank[:, :], xT[0][:, d, :].bitcast(F32), ALU.subtract),
                  [("xhi", d)], ("xlo", d), 0)

        PRODUCTS = ((0, 0), (0, 1), (1, 0))

        def ready_x(u):
            return [("prev", ("xlo", KD - 1)) if u else ("xlo", KD - 1)]

        def project(n, u, stage):
            def fn(e, it, bank):
                for i, (d, (pw, px)) in enumerate((d, pr) for d in range(KD) for pr in PRODUCTS):
                    ins = e.matmul(bank[:, :], w[n][pw][:, d, u * P:(u + 1) * P], xT[px][:, d, :],
                                   start=(i == 0), stop=(i == KD * len(PRODUCTS) - 1))
                return ins
            bank = job(fn, ready_x(u), (n, "proj", u), (n, "raw", u), stage)
            ph.op("scalar", lambda e, it: e.activation(raw[n][:, :], bank[:, :], ACT.Copy), [(n, "proj", u)], (n, "raw", u), stage)
            ph.op("gpsimd", lambda e, it: e.tensor_tensor(work_qk[n][:, :], raw[n][:, :], raw[n][:, :], ALU.mult),
                  [(n, "raw", u), ("prev", (n, "lo", 0)) if u else (n, "lo", 1)], (n, "sq", u), stage)

        def rms(n, u, stage):
            bank = job(lambda e, it, bank: e.matmul(bank[:, :], headsum[:, :], work_qk[n][:, :], start=True, stop=True),
                       [(n, "sq", u)], (n, "ms", u), (n, "ln", u), stage)
            ph.op("scalar", lambda e, it: e.activation(work_qk[n][:, :], bank[:, :], ACT.Ln, bias=eps_rms[:, 0:1], scale=1.0 / DH),
                  [(n, "ms", u)], (n, "ln", u), stage)
            ph.op("scalar", lambda e, it: e.activation(work_qk[n][:, :], work_qk[n][:, :], ACT.Exp, scale=-0.5),
                  [(n, "ln", u)], (n, "inv", u), stage)

        def parts(n, u, stage):
            weight = wq_scale[:, 0:1] if n == "q" else 1.0
            ph.op("vector", lambda e, it: e.scalar_tensor_tensor(work_qk[n][:, :], raw[n][:, :], weight, work_qk[n][:, :], ALU.mult, ALU.mult),
                  [(n, "inv", u)], (n, "full", u), stage)
            def other(*step):
                return ("prev", (*step, 0)) if u else (*step, 1)
            ph.op("vector", lambda e, it: e.tensor_copy(part[n][0][:, :], work_qk[n][:, :]),
                  [(n, "full", u), other(n, "out0")], (n, "hi", u), stage)
            ph.op("gpsimd", lambda e, it: e.tensor_tensor(part[n][1][:, :], work_qk[n][:, :], part[n][0][:, :].bitcast(F32), ALU.subtract),
                  [(n, "hi", u), other(n, "out1")], (n, "lo", u), stage)

        def part_out(n, p, u, stage):
            ph.dma("sync", [lambda e, it: e.dma_start(parts_dram[u, "qk".index(n), p], part[n][p][:, :].bitcast(F32))],
                   [(n, ("hi", "lo")[p], u), ("prev", (n, f"stack{p}", u))], (n, f"out{p}", u), stage)

        def part_in(n, p, u, stage):
            order = (0, 0, 1) if n == "q" else (0, 1, 0)
            src = parts_dram[u, "qk".index(n), p].rearrange("(h d) n -> d h n", d=DH)
            free = ("prev", ("qk_done", u)) if u == 1 or stage else ("qk_done", u)
            ph.dma("sync", [lambda e, it, r=r: e.dma_start(stack[n][u][r * DH:(r + 1) * DH, :, :].bitcast(F32), src)
                            for r in range(3) if order[r] == p],
                   [(n, f"out{p}", u), free], (n, f"stack{p}", u), stage)

        def stacked(u):
            steps = [(n, f"stack{p}", u) for n in "qk" for p in range(2)]
            return steps if u else [("prev", x) for x in steps]

        def project_v(i):
            def fn(e, it, bank):
                for c in range(2):
                    at = (2 * i + c) * P
                    for n, (d, (px, pw)) in enumerate((d, pr) for d in range(KD) for pr in PRODUCTS):
                        ins = e.matmul(bank[:, c * D:(c + 1) * D], xT[px][:, d, at:at + P], w["v"][pw][:, d, :],
                                       start=(n == 0), stop=(n == KD * len(PRODUCTS) - 1))
                return ins
            bank = job(fn, [("xlo", KD - 1)], ("vproj", i), ("v", 0, i), 0)
            seen = bank[:, :].rearrange("p (c d) -> p c d", c=2)
            ph.op("vector", lambda e, it: e.tensor_copy(v_next[:, 2 * i:2 * i + 2, :], seen[:, :, P:D]),
                  [("vproj", i), ("v", 1)], ("vnext", i), 0)
            ph.op("vector", lambda e, it: e.tensor_copy(
                v[0][:, 2 * i:2 * i + 2, :, 0:DH], seen[:, :, 0:P].rearrange("p c (h d) -> p c h d", h=HU)),
                [("vproj", i), ("pv_done", 0)], ("v", 0, i), 0)

        def second_v():
            ph.op("gpsimd", lambda e, it: e.tensor_copy(
                v[1][:, :, :, 0:DH], v_next[:, :, :].rearrange("p c (h d) -> p c h d", h=HU)),
                [("prev", ("vnext", 1)), ("pv_done", 1)], ("v", 1), 1)

        s_g = {n: ctx.enter_context(nc.semaphore(f"g_{n}")) for n in ("mm", "red", "neg", "tp", "sh", "dma")}
        needed = {}

        def shift(u):
            pairs = HU * CH // 2

            def n_of(it):
                return 2 * it + u

            def pe(e, it):
                for i in range(pairs):
                    h, c0 = i // 2, 2 * (i % 2)
                    if i >= 2:
                        e.wait_ge(s_g["red"], pairs * n_of(it) + i - 1)
                    for c in range(2):
                        ins = e.matmul(S[i % 2][:, c, :], stack["q"][u][0:3 * DH, h, (c0 + c) * P:(c0 + c + 1) * P],
                                       stack["k"][u][0:3 * DH, h, :], start=True, stop=True)
                    ins.then_inc(s_g["mm"], 1)
                e.wait_ge(s_g["neg"], n_of(it) + 1)
                e.transpose(S[0][0:HU * CH, 0, 0:P], mx[:, :], k["ident"][:, :]).then_inc(s_g["tp"], 1)
                e.wait_ge(s_g["sh"], 3 * n_of(it) + 3)
                e.wait_ge(s_g["dma"], 64 * n_of(it) + 64)

            def dve(e, it):
                for i in range(pairs):
                    e.wait_ge(s_g["mm"], pairs * n_of(it) + i + 1)
                    e.tensor_reduce(mx[:, 2 * i:2 * i + 2], S[i % 2][:, :, :], AX.X, ALU.max).then_inc(s_g["red"], 1)
                e.wait_ge(s_g["red"], pairs * n_of(it) + pairs)
                e.tensor_scalar(mx[:, :], mx[:, :], -1.0, None, ALU.mult).then_inc(s_g["neg"], 1)
                e.wait_ge(s_g["tp"], n_of(it) + 1)
                e.tensor_copy(shf[:, :], S[0][0:HU * CH, 0, 0:P]).then_inc(s_g["sh"], 1)
                e.wait_ge(s_g["sh"], 3 * n_of(it) + 1)
                e.tensor_copy(sh[0][:, :], shf[:, :]).then_inc(s_g["sh"], 1)
                e.wait_ge(s_g["sh"], 3 * n_of(it) + 2)
                e.tensor_tensor(sh[1][:, :], shf[:, :], sh[0][:, :].bitcast(F32), ALU.subtract).then_inc(s_g["sh"], 1)

            def sp(e, it):
                e.wait_ge(s_g["sh"], 3 * n_of(it) + 3)
                e.nop(nofuse=True)
                for i in range(2):
                    e.dma_start(shift_dram[i], sh[i][:, :].bitcast(F32)).then_inc(s_g["dma"], 16)
                e.wait_ge(s_g["dma"], 64 * n_of(it) + 32)
                e.nop(nofuse=True)
                for i in range(2):
                    r = ROW_SHIFT + i
                    e.dma_start(stack["q"][u][r:r + 1, :, :].bitcast(F32),
                                shift_dram[i].rearrange("(o h c) q -> o h (c q)", o=1, h=HU)).then_inc(s_g["dma"], 16)
                e.wait_ge(s_g["dma"], 64 * n_of(it) + 64)
                e.nop(nofuse=True)

            def only(eng, fn):
                def run(e, it):
                    with e.If(needed[eng] > 0):
                        fn(e, it)
                    return None
                return run
            before = stacked(u)
            exp_before = ("exp", 3, G - 1) if u else ("prev", ("exp", 7, G - 1))
            ph.op("tensor", only("tensor", pe), [*before, exp_before])
            ph.op("vector", only("vector", dve))
            ph.op("sync", only("sync", sp))

        def heads(s, j):
            u, g, half = s // 4, s % 4 // 2, s % 2
            h = G * g + j
            n = G * s + j
            free = [("exp", (n - 2) // G, (n - 2) % G)] if n >= 2 else [("prev", ("exp", 7, G - 2 + n))]

            def fn(e, it):
                for c in range(2):
                    key = 2 * half + c
                    ins = e.matmul(S[j % 2][:, c, :], stack["k"][u][:, h, key * P:(key + 1) * P],
                                   stack["q"][u][:, h, :], start=True, stop=True)
                return ins
            key = ("qk_done", u) if (s % 4 == 3 and j == G - 1) else ("qk", s, j)
            ph.op("tensor", fn, [*stacked(u), *free], key)
            freed = [("pv", s - 2, 1)] if s >= 2 else [("prev", ("pv", 6, 1)) if s == 0 else ("pv_done", 1)]
            freed = [x if x != ("pv", 3, 1) else ("pv_done", 0) for x in freed]
            ph.op("scalar", lambda e, it: e.activation(prob[s % 2][:, j, :, :], S[j % 2][:, :, :], ACT.Exp),
                  [key, *freed], ("exp", s, j))

        def weigh(s, c):
            u, g, half = s // 4, s % 4 // 2, s % 2

            def fn(e, it):
                for j in range(G):
                    ins = e.matmul(pv[VW * j:VW * (j + 1), :], v[u][:, 2 * half + c, G * g + j, :],
                                   prob[s % 2][:, j, c, :], start=(half == 0 and c == 0), stop=(half == 1 and c == 1))
                return ins
            q = s // 2
            stage = 2 if s == 7 else 1
            if s == 7:
                after = [("prev", ("exp", s, G - 1)), ("prev", ("v", 1))]
            else:
                after = [("exp", s, G - 1), ("v", 1) if u else ("prev", ("v", 0, 1))]
            if half == 0 and c == 0:
                after.append(("pvcopy", q - 1) if q else ("pvcopy", 3))
            key = ("pv_done", u) if (s % 4 == 3 and c == 1) else ("pv", s, c)
            ph.op("tensor", fn, after, key, stage)
            if half == 1 and c == 1:
                turned_before = {0: ("prev", ("oturn", 2)), 1: ("oturn", 3), 2: ("oturn", 0), 3: ("prev", ("oturn", 1))}[q]
                ph.op("vector", lambda e, it: e.tensor_copy(oT[q % 2][:, :], pv[:, :]), [key, turned_before], ("pvcopy", q), stage)

        def normalise(q, stage=1):
            def fn(e, it, bank):
                for c in range(CH):
                    ins = e.transpose(bank[:, c * P:(c + 1) * P], oT[q % 2][:, c * P:(c + 1) * P], k["ident"][:, :])
                return ins
            bank = job(fn, [("pvcopy", q)], ("oturn", q), ("onorm", q), stage)
            seen = bank[:, :].rearrange("p (c j w) -> p c j w", c=CH, j=G)
            r = rden[q % 2]
            ph.op("vector", lambda e, it: e.reciprocal(r[:, :, :], seen[:, :, :, DH]), [("oturn", q)], ("rden", q), stage)
            free = [("o2turn", KD - 1)] if q == 0 else []
            ph.op("vector", lambda e, it: e.tensor_tensor(
                o_tok[:, :, G * DH * q:G * DH * (q + 1)].rearrange("p c (j d) -> p c j d", j=G),
                seen[:, :, :, 0:DH], r[:, :, :].unsqueeze(3).broadcast_to([P, CH, G, DH]), ALU.mult),
                [("rden", q), *free], ("onorm", q), stage)

        def turn_o(d):
            def fn(e, it, bank):
                for c in range(CH):
                    ins = e.transpose(bank[:, c * P:(c + 1) * P], o_tok[:, c, d * P:(d + 1) * P], k["ident"][:, :])
                return ins
            bank = job(fn, [("onorm", 3)], ("o2turn", d), ("o2", d), 2)
            ph.op("scalar", lambda e, it: e.activation(oT2[:, d, :], bank[:, :], ACT.Copy),
                  [("o2turn", d), ("prev", ("wo", 1))], ("o2", d), 2)

        def project_o(i):
            def fn(e, it, bank):
                for c in range(2):
                    for d in range(KD):
                        ins = e.matmul(bank[:, c * D:(c + 1) * D], oT2[:, d, (2 * i + c) * P:(2 * i + c + 1) * P],
                                       wo[:, d, :], start=(d == 0), stop=(d == KD - 1))
                return ins
            bank = job(fn, [("o2", KD - 1)], ("wo", i), ("woe", i), 2)
            ph.op("vector", lambda e, it: e.tensor_tensor(
                ao[:, 2 * i:2 * i + 2, :], bank[:, :].rearrange("p (c d) -> p c d", c=2), ao[:, 2 * i:2 * i + 2, :], ALU.add),
                [("wo", i), ("prev", ("aosum",))], ("woe", i), 2)
            if i == 1:
                ph.dma("sync", [lambda e, it: e.dma_start(row_batch[it - 1][:, :, D:2 * D], ao[:, :, :])],
                    [("woe", 0), ("woe", 1)], ("attn",), 2)

        def on_score(eng, fn, after, key):
            ph.op(eng, fn, after, key, 1, "score")

        def score_steps(j):
            f, tiles = feat[j % 3], tiles_feat[j % 2]
            one = LayerNorm(ph, f"f{j}", f, tiles[0], k, f, 1, "score")
            two = LayerNorm(ph, f"g{j}", f, tiles[1], k, f, 1, "score")

            def last(key, at):
                return (key, j - at) if j >= at else ("prev", (key, j - at + SCORED))

            def load():
                free = ("fturned", 0) if j == 3 else ("prev", ("fturned", j if j else 3))
                ph.dma("sync", [lambda e, it: e.dma_start(f[:, :, :], x_batch[SCORED * (it - FIRST["score"]) + j])],
                       [free] + ([("prev", ("fturned", 0))] if j == 0 else []), ("feat", j), 1, "score")

            def first_norm():
                tag = f"f{(j - 2) % SCORED}"
                one.moments([("feat", j)], [(tag, "out") if j >= 2 else ("prev", (tag, "out"))])

            def second_norm():
                one.scale()
                tag = f"g{(j - 2) % SCORED}"
                two.moments([(f"f{j}", "out")], [(tag, "out") if j >= 2 else ("prev", (tag, "out"))])

            def turn(d):
                def fn(e, it):
                    for c in range(CH):
                        ins = e.transpose(R[:, c * P:(c + 1) * P], f[:, c, d * P:(d + 1) * P], k["ident"][:, :])
                    return ins
                free = ("gained", j, 0) if d else last("keep", 1)
                on_score("tensor", fn, [(f"g{j}", "out"), free], ("fturned", j) if d else ("fturn", j))
                on_score("scalar", lambda e, it: e.activation(
                    featT[:, d, :], R[:, :], ACT.Identity, bias=k["offset"][:, d:d + 1], scale=k["gain"][:, d:d + 1]),
                    [("fturned", j) if d else ("fturn", j), last("scored", 1)], ("gained", j, d))

            def score():
                def fn(e, it):
                    for c in range(CH):
                        for d in range(KD):
                            ins = e.matmul(R[:, c * E:(c + 1) * E], featT[:, d, c * P:(c + 1) * P], cent[:, d, :],
                                           start=(d == 0), stop=(d == KD - 1))
                    return ins
                on_score("tensor", fn, [("gained", j, KD - 1)], ("scored", j))
                on_score("vector", lambda e, it: e.tensor_copy(
                    scores[:, :, bass.ds(CH * (SCORED * (it - FIRST["score"]) + j), CH)].rearrange("p e c -> p c e"),
                    R[:, 0:CH * E].rearrange("p (c e) -> p c e", c=CH)), [("scored", j)], ("keep", j))
            return load, [first_norm, second_norm, lambda: two.scale(), lambda: turn(0), lambda: turn(1), score]

        def expert(it):
            return it - FIRST["route"]

        def route(fn, eng="vector", after=(), key=None):
            ph.op(eng, fn, after, key, 1, "route")

        def bits_ask(i):
            if i == 0:
                def start(e, it):
                    e.wait_ge(*ph.value(("keep", SCORED - 1), FIRST["route"] - 1))
                    return e.memset(zcur[:, :], -2 ** 31)
                route(start, after=[("prev", ("r_taken",))], key=("r_init",))
                route(lambda e, it: e.tensor_tensor(zc[:, :], zcur[:, :].broadcast_to([P, CAND]), cand_bits[:, i, :], ALU.bitwise_xor),
                      after=[("r_init",)], key=("r_zc",))
                route(lambda e, it: e.tensor_scalar(sgn[:, :], zc[:, :], 31, 1, ALU.arith_shift_right, ALU.logical_shift_right),
                      after=[("r_zc",)], key=("r_sg",))
                route(lambda e, it: e.tensor_tensor(thr[:, :], zc[:, :], sgn[:, :], ALU.bitwise_xor),
                      after=[("r_sg",)], key=("r_th", i))
            else:
                route(lambda e, it: e.tensor_tensor(thr[:, :], best[:, :].broadcast_to([P, CAND]), cand_bits[:, i, :], ALU.bitwise_xor),
                      after=[("r_z", i - 1)], key=("r_th", i))

            route(lambda e, it: e.tensor_tensor(
                ge[:, :, :], scores[:, bass.ds(expert(it), 1), :].broadcast_to([P, CAND, NT]),
                thr[:, :].bitcast(F32).unsqueeze(2).broadcast_to([P, CAND, NT]), ALU.is_ge),
                after=[("r_th", i)], key=("r_ge", i))
            route(lambda e, it: e.tensor_reduce(part_cnt[:, :], ge[:, :, :], AX.X, ALU.add),
                  after=[("r_ge", i)], key=("r_pc", i))

        def bits_answer(i):
            route(lambda e, it: e.matmul(R[:, 0:CAND], ones_h[:, :], part_cnt[:, :], start=True, stop=True),
                  "tensor", [("r_pc", i)], ("r_cnt", i))
            route(lambda e, it: e.tensor_scalar(gem[:, :], R[:, 0:CAND], float(C), None, ALU.is_ge, ALU.add, accum_out=digit[:, :]),
                  after=[("r_cnt", i)], key=("r_dg", i))
            route(lambda e, it: e.tensor_scalar(zadd[:, :], digit[:, :], steps_f[:, i:i + 1], None, ALU.mult),
                  after=[("r_dg", i)], key=("r_za", i))
            held = best if i else zcur
            route(lambda e, it: e.tensor_tensor(held[:, :], held[:, :], zadd[:, :].bitcast(I32), ALU.bitwise_xor),
                  after=[("r_za", i)], key=("r_zz", i) if i == 0 else ("r_z", i))
            if i == 0:
                route(lambda e, it: e.tensor_scalar(mask[:, :], zcur[:, :], 31, 1, ALU.arith_shift_right, ALU.logical_shift_right),
                      after=[("r_zz", 0)], key=("r_mask",))
                route(lambda e, it: e.tensor_tensor(best[:, :], zcur[:, :], mask[:, :], ALU.bitwise_xor),
                      after=[("r_mask",)], key=("r_z", 0))

        def ranks(src, after, key):
            def fn(e, it):
                e.matmul(R[:, NT:2 * NT], below[:, :], src[:, :], start=True, stop=True)
                return e.matmul(R[:, 2 * NT:3 * NT], ones_h[:, :], src[:, :], start=True, stop=True)
            route(fn, "tensor", after, (key, "mm"))

        def rank_rows(key):
            route(lambda e, it: e.tensor_copy(cols[:, :], R[:, 2 * NT:3 * NT]), after=[(key, "mm")], key=(key, "col"))
            route(lambda e, it: e.tensor_tensor_scan(csum[:, :], cols[:, :], zero[:, :], 0.0, ALU.add, ALU.add),
                  after=[(key, "col")], key=(key, "scan"))
            route(lambda e, it: e.tensor_tensor(csum[:, :], csum[:, :], cols[:, :], ALU.subtract),
                  after=[(key, "scan")], key=(key, "before"))

        def choose():
            last = STEPS - 1
            def flags(dst, op):
                return lambda e, it: e.tensor_tensor(dst[:, :], scores[:, bass.ds(expert(it), 1), :].rearrange("p o t -> p (o t)"),
                                                     best[:, :].bitcast(F32).broadcast_to([P, NT]), op)
            route(flags(gt, ALU.is_gt), after=[("r_z", STEPS - 1)], key=("c_gt",))
            route(flags(eq, ALU.is_equal), key=("c_eq",))
            route(lambda e, it: e.tensor_reduce(gt_cnt[:, :], gt[:, :], AX.X, ALU.add), after=[("c_gt",)], key=("c_gc",))

        def missing():
            route(lambda e, it: e.matmul(R[:, 0:1], ones_h[:, :], gt_cnt[:, :], start=True, stop=True), "tensor", [("c_gc",)], ("c_gn",))
            route(lambda e, it: e.tensor_scalar(need[:, :], R[:, 0:1], -1.0, float(C), ALU.mult, ALU.add), after=[("c_gn",)], key=("c_need",))

        def ties():
            ranks(eq, [("c_eq",), ("c_need",)], "tie")

        def choose_ties():
            rank_rows("tie")
            route(lambda e, it: e.tensor_tensor(rank[:, :], R[:, NT:2 * NT], csum[:, :], ALU.add), after=[("tie", "before")], key=("c_rank",))
            route(lambda e, it: e.scalar_tensor_tensor(tie[:, :], rank[:, :], need[:, 0:1], eq[:, :], ALU.is_lt, ALU.mult),
                  after=[("c_rank",)], key=("c_tie",))
            route(lambda e, it: e.tensor_tensor(sel[:, :], gt[:, :], tie[:, :], ALU.add), after=[("c_tie",)], key=("c_sel",))
            route(lambda e, it: e.tensor_copy(sel_i[:, :], sel[:, :]), after=[("c_sel",)], key=("c_seli",))

        def place():
            rank_rows("slot")
            route(lambda e, it: e.tensor_tensor(rank2[:, :], R[:, NT:2 * NT], csum[:, :], ALU.add), after=[("slot", "before")], key=("p_rank",))
            route(lambda e, it: e.scalar_tensor_tensor(rank2[:, :], rank2[:, :], base[:, 0:1], sel[:, :], ALU.add, ALU.mult),
                  after=[("p_rank",)], key=("p_slot",))
            route(lambda e, it: e.tensor_tensor(slot[:, :], slot[:, :], rank2[:, :], ALU.add), after=[("p_slot",)], key=("p_sum",))
            route(lambda e, it: e.tensor_scalar(base[:, :], base[:, :], float(C), None, ALU.add), key=("p_base",))
            ph.apart.add(("r_taken",))
            route(lambda e, it: e.copy_predicated(
                scores[:, :, :], sel_i[:, :].unsqueeze(1).broadcast_to([P, E, NT]),
                lowest[:, :].unsqueeze(1).broadcast_to([P, E, NT])),
                after=[("p_base",)], key=("r_taken",))

        def order_tiles():
            def order_op(eng, fn, after, key):
                ph.op(eng, fn, after, key, 1, "order")

            def now(e, it):
                e.wait_ge(*ph.value(("p_sum",), FIRST["order"] - 1))
                return e.tensor_copy(slot_now[:, :], slot[:, bass.ds(ORDERED * (it - FIRST["order"]), ORDERED)])
            order_op("vector", now, [], ("now",))
            order_op("vector", lambda e, it: e.tensor_scalar(place_p[:, :], slot_now[:, :], P - 1, NT.bit_length() - 1,
                                                             ALU.bitwise_and, ALU.logical_shift_left), [("now",)], ("place_p",))
            order_op("vector", lambda e, it: e.tensor_scalar(place_t[:, :], slot_now[:, :], P.bit_length() - 1, None,
                                                             ALU.logical_shift_right), [], ("place_t",))
            order_op("vector", lambda e, it: e.tensor_tensor(placed[:, :], place_p[:, :], place_t[:, :], ALU.bitwise_or),
                     [("place_t",), ("prev", ("order_done",))], ("place",))
            order_op("gpsimd", lambda e, it: e.tensor_copy(
                token_now[:, :], k["tokens"][:, bass.ds(ORDERED * (it - FIRST["order"]), ORDERED)]), [("place",)], ("token",))

        def order_tile(t):
            ph.dma("gpsimd", [lambda e, it: e.indirect_dma_start(
                out=order_dram, out_offset=bass.IndirectOffsetOnAxis(ap=placed[:, t:t + 1], axis=0),
                in_=token_now[:, t:t + 1], in_offset=None)], [("token",)], ("order", t), 1, "order")

        def order_done():
            ph.op("gpsimd", lambda e, it: e.nop(nofuse=True), [("order", t) for t in range(ORDERED)], ("order_done",), 1, "order")

        def unit(u, stage, at):
            return [(at, lambda: project("q", u, stage)), (at, lambda: project("k", u, stage)),
                    (at + 1, lambda: rms("q", u, stage)), (at + 2, lambda: rms("k", u, stage)),
                    (at + 2, lambda: parts("q", u, stage)),
                    (at + 2, lambda: [part_out("q", 0, u, stage), part_out("q", 1, u, stage), part_in("q", 0, u, stage)]),
                    (at + 3, lambda: parts("k", u, stage)),
                    (at + 3, lambda: [part_out("k", 0, u, stage), part_in("q", 1, u, stage), part_out("k", 1, u, stage),
                                      part_in("k", 0, u, stage), part_in("k", 1, u, stage)])]

        work = unit(1, 1, 0) + unit(0, 0, 8) + [
            (0, load_x), (2, second_v), (2, lambda: normalise(3, 2)),
            (3, lambda: turn_o(0)), (3, lambda: turn_o(1)), (3, lambda: norm.moments([("xload",)])),
            (4, lambda: project_o(0)), (4, norm_x), (5, lambda: project_o(1)),
            (6, lambda: turn_x(0)), (7, lambda: turn_x(1)),
            (7, lambda: normalise(0)), (11, lambda: normalise(1)), (15, lambda: normalise(2)),
            (13, lambda: project_v(0)), (14, lambda: project_v(1)), (14, keep_sum),
            (0, order_tiles)] + [(t * 13 // ORDERED, lambda t=t: order_tile(t)) for t in range(ORDERED)] + [(15, order_done)]
        score_first = [1, 4, 7, 10]
        for j, at in enumerate(score_first):
            load, steps = score_steps(j)
            work += [(0 if j < 3 else 6, load)] + [(at + i, step) for i, step in enumerate(steps)]
        ROUTE_POINTS = [0, 1, 2, 3, 5, 6, 7, 8, 9, 10, 11, 12, 13, 14, 15]
        ask_steps = [lambda i=i: bits_ask(i) for i in range(STEPS)] + [choose, None, choose_ties, place]
        answer_steps = [lambda i=i: bits_answer(i) for i in range(STEPS)] + [
            missing, ties, lambda: ranks(sel, [("c_sel",)], "slot"), None]
        assert len(ROUTE_POINTS) == len(ask_steps)
        ask = {at: fn for at, fn in zip(ROUTE_POINTS, ask_steps) if fn}
        answer = {at: fn for at, fn in zip(ROUTE_POINTS, answer_steps) if fn}

        for s in range(8):
            if s % 4 == 0:
                shift(s // 4)
            for half in range(2):
                point = 2 * s + half
                ask.get(point, lambda: None)()
                heads(s, 2 * half)
                heads(s, 2 * half + 1)
                weigh(s - 1 if s else 7, half)
                for at, fn in work:
                    if at == point:
                        fn()
                answer.get(point, lambda: None)()
        assert len(job_release) % 2 == 0 and job_release[-2:] == job_release_tail, job_release

        with nc.Block() as block:
            def program_for(eng):
                def program(e):
                    setup[eng](e)
                    if eng in ("tensor", "vector", "sync"):
                        needed[eng] = e.value_load(flag[0:1, 0:1], min_val=0, max_val=1)
                    ph.credit(eng, e)
                    for its, stages, groups in plan:
                        if eng == "sync" and its == B:
                            for t in range(ORDERED):
                                e.wait_ge(*ph.value(("order", t), B - 1))
                            e.dma_start(k["order"][:, :, :, :].rearrange("p e u c -> p (e u c)"),
                                        order_dram.rearrange("(p t) o -> p (t o)", p=P)).then_inc(s_order, 16)
                        if isinstance(its, int):
                            ph.body(eng, e, its, stages, groups)
                        else:
                            with e.Fori(its[0], its[1]) as it:
                                ph.body(eng, e, it, stages, groups)
                    if eng == "sync":
                        e.wait_ge(*ph.value(("attn",), B))
                        e.wait_ge(*ph.value(("xrow",), B - 2))
                        e.wait_ge(s_order, 16)
                return program
            score, route_, order = {"", "score"}, {"", "route"}, {"", "order"}
            plan = [(-1, {0}, {""}), (0, {0, 1}, score), ((1, FIRST["route"]), {0, 1, 2}, score),
                    ((FIRST["route"], FIRST["order"]), {0, 1, 2}, route_),
                    ((FIRST["order"], B - 1), {0, 1, 2}, order), (B - 1, {1, 2}, order), (B, {2}, {""})]
            setup = {"sync": setup_sync, "scalar": setup_scalar, "vector": setup_vector,
                     "gpsimd": setup_gpsimd, "tensor": setup_tensor}
            for eng in ("sync", "scalar", "vector", "gpsimd", "tensor"):
                on_engine(block, eng)(program_for(eng))


def experts(nc, a, rows_dram, out, k):
    U = 2
    UP = 4
    assert C == U * N and NFC % UP == 0 and CH == 4
    with ExitStack() as ctx:
        def sb(name, shape, dt=F32):
            return ctx.enter_context(nc.sbuf_tensor(name, shape, dt))

        w1raw = sb("w1raw", [P, KD, F])
        w2raw = sb("w2raw", [P, NFC, D])
        w1 = [sb(f"w1_{i}", [P, KD, F], F32R) for i in range(2)]
        w2 = [sb(f"w2_{i}", [P, NFC, D], F32R) for i in range(2)]
        b1 = sb("b1", [P, E, NFC])
        b2_now = [sb(f"b2_now{u}", [P, D]) for u in range(U)]
        order = k["order"]
        rows = [sb(f"rows{u}", [P, CH], I32) for u in range(U)]
        rows_in = [sb(f"rows_in{u}", [P, CH], I32) for u in range(U)]
        g = [sb(f"g{u}", [P, CH, 2 * D]) for u in range(U)]
        z = sb("e_z", [P, CH, D])
        nf = sb("nf", [P, KD, N])
        nT = [[sb(f"nT{u}{i}", [P, KD, N], F32R) for i in range(2)] for u in range(U)]
        act = [sb(f"act{i}", [P, N]) for i in range(UP)]
        hid = [sb(f"hid{i}", [P, NFC, N], F32R) for i in range(2)]
        y = [sb(f"y{u}", [P, CH, D]) for u in range(U)]
        stats, aggr, veps, rstd, nmean, shift = (
            sb(f"e_{n}", s) for n, s in (("st", [P, CH, 6]), ("mv", [P, CH, 2]), ("ve", [P, CH]), ("rs", [P, CH]),
                                         ("nm", [P, CH]), ("sh", [P, CH])))
        up = [ctx.enter_context(nc.psum_tensor(f"up{i}", [P, N], F32)) for i in range(UP)]
        turned = [ctx.enter_context(nc.psum_tensor(f"tu{i}", [P, N], F32)) for i in range(KD)]
        down = [ctx.enter_context(nc.psum_tensor(f"dn{i}", [P, N], F32)) for i in range(2)]
        PRODUCTS = ((0, 0), (0, 1), (1, 0))

        s_b1 = ctx.enter_context(nc.semaphore("e_b1"))

        def load_constants(e):
            e.dma_start(b1[:, :, :], a["b1"]).then_inc(s_b1, 16)

        ph = Phase(nc, "e", ctx)

        def ex(it, stage):
            return it + 1 - stage

        def load_weights(name, land, src):
            last = (name, "lo", SPLITS - 1)
            ph.dma("sync", [lambda e, it: e.dma_start(land[:, :, :], src[ex(it, 0)])],
                   [last, ("gather", 0, CH - 1)] if name == "w2" else [("prev", last)], (name, "raw"), 0)

        SPLITS = 4
        raw = {"w1": w1raw, "w2": w2raw}
        parts = {"w1": w1, "w2": w2}

        def split_piece(name, i):
            hi, lo = parts[name]
            src = raw[name]
            stage = 1 if name == "w2" else 0
            n = F * KD // SPLITS if name == "w1" else NFC // SPLITS
            if name == "w1":
                d, at = i // 2, slice(i % 2 * n, (i % 2 + 1) * n)
                pick = lambda t: t[:, d, at]
            else:
                pick = lambda t: t[:, i * n:(i + 1) * n, :]
            loaded = (name, "raw") if name == "w1" else ("prev", (name, "raw"))
            used = ("up", 1, NFC - 1) if name == "w1" else ("prev", ("down", 1, CH - 1))
            ph.op("scalar", lambda e, it: e.activation(pick(hi), pick(src), ACT.Copy), [loaded, used], (name, "hi", i), stage)
            ph.op("vector", lambda e, it: e.tensor_tensor(pick(lo), pick(src), pick(hi).bitcast(F32), ALU.subtract),
                  [(name, "hi", i)], (name, "lo", i), stage)

        def load_bias(u):
            ph.dma("sync", [lambda e, it: e.dma_start(
                b2_now[u][:, :], a["b2"].rearrange("(o e) d -> e o d", o=1)[ex(it, 0)].broadcast_to([P, D]))],
                [("bias", 1) if u else ("prev", ("bias", 0))], ("b2", u), 0)

        def next_rows(u):
            def fn(e, it):
                return e.tensor_copy(rows[u][:, :], rows_in[u][:, :])
            ph.op("gpsimd", fn, [("prev", ("gather", u, CH - 1)), *[("prev", ("scatter", u, c)) for c in range(CH)]], ("rows", u), 1)
            ph.op("gpsimd", lambda e, it: e.tensor_copy(rows_in[u][:, :], order[:, bass.ds(ex(it, 0), 1), u, :].rearrange("p o c -> p (o c)")),
                  [("rows", u), *[("prev", ("gather", u, c)) for c in range(CH)]], ("rows_in", u), 0)

        def gather(u, c):
            ph.dma("gpsimd", [lambda e, it: e.indirect_dma_start(
                out=g[u][:, c, :], out_offset=None, in_=rows_dram,
                in_offset=bass.IndirectOffsetOnAxis(ap=rows_in[u][:, c:c + 1], axis=0))],
                [("rows_in", u), ("y", u, c)], ("gather", u, c), 0)

        def other(u, *step):
            return ("prev", step) if u else step

        def gathered(u, c):
            return ("prev", ("gather", u, c)) if u else ("gather", u, c)

        def prepare(u):
            stage = u
            pieces = {}

            def stat(c):
                ph.op("vector", lambda e, it: e.bn_stats(stats[:, c, :], g[u][:, c, 0:D]),
                      [gathered(u, c), other(u, "aggr", 1 - u)], ("stat", u, c), stage)

            def aggregate():
                def fn(e, it):
                    for c in range(CH):
                        ins = e.bn_aggr(aggr[:, c, :], stats[:, c, :])
                    return ins
                ph.apart.add(("aggr", u))
                ph.op("vector", fn, [("stat", u, CH - 1), other(u, "shift", 1 - u)], ("aggr", u), stage)
                ph.op("gpsimd", lambda e, it: e.tensor_tensor(veps[:, :], aggr[:, :, 1], k["eps_ln"][:, :], ALU.add),
                      [("aggr", u)], ("veps", u), stage)
                ph.op("gpsimd", lambda e, it: e.tensor_tensor(nmean[:, :], aggr[:, :, 0], k["minus"][:, :], ALU.mult),
                      [other(u, "shift", 1 - u)], ("nmean", u), stage)
                ph.op("gpsimd", lambda e, it: e.tensor_tensor(rstd[:, :], veps[:, :], k["half"][:, :], ALU.pow),
                      [("veps", u), other(u, "scale", 1 - u), other(u, "scale_v", 1 - u)], ("rstd", u), stage)
                ph.op("gpsimd", lambda e, it: e.tensor_tensor(shift[:, :], nmean[:, :], rstd[:, :], ALU.mult),
                      [("rstd", u)], ("shift", u), stage)

            def scale():
                def on_scalar(e, it):
                    for c in range(CH // 2):
                        ins = e.activation(z[:, c, :], g[u][:, c, 0:D], ACT.Identity, bias=shift[:, c:c + 1], scale=rstd[:, c:c + 1])
                    return ins

                def on_vector(e, it):
                    for c in range(CH // 2, CH):
                        ins = e.tensor_scalar(z[:, c, :], g[u][:, c, 0:D], aggr[:, c, 0:1], rstd[:, c:c + 1], ALU.subtract, ALU.mult)
                    return ins
                ph.op("scalar", on_scalar, [("shift", u), other(u, "turn", 1 - u, KD - 1)], ("scale", u), stage)
                ph.op("vector", on_vector, [("rstd", u), other(u, "turn", 1 - u, KD - 1)], ("scale_v", u), stage)

            def add_bias():
                ph.op("gpsimd", lambda e, it: e.tensor_tensor(
                    g[u][:, :, D:2 * D], g[u][:, :, D:2 * D], b2_now[u][:, :].unsqueeze(1).broadcast_to([P, CH, D]), ALU.add),
                    [("prev", ("b2", 1)) if u else ("b2", 0), gathered(u, CH - 1)], ("bias", u), stage)

            def turn(d):
                def fn(e, it):
                    for c in range(CH):
                        ins = e.transpose(turned[d][:, c * P:(c + 1) * P], z[:, c, d * P:(d + 1) * P], k["ident"][:, :])
                    return ins
                ph.op("tensor", fn, [("scale", u), ("scale_v", u), other(u, "affine", 1 - u, d)], ("turn", u, d), stage)
                ph.op("scalar", lambda e, it: e.activation(nf[:, d, :], turned[d][:, :], ACT.Identity,
                                                           bias=k["offset"][:, d:d + 1], scale=k["gain"][:, d:d + 1]),
                      [("turn", u, d), other(u, "nlo", 1 - u, d)], ("affine", u, d), stage)
                ph.op("vector", lambda e, it: e.tensor_copy(nT[u][0][:, d, :], nf[:, d, :]),
                      [("affine", u, d), ("up", u, NFC - 1) if u == 0 else ("prev", ("up", u, NFC - 1))], ("nhi", u, d), stage)
                ph.op("vector", lambda e, it: e.tensor_tensor(nT[u][1][:, d, :], nf[:, d, :], nT[u][0][:, d, :].bitcast(F32), ALU.subtract),
                      [("nhi", u, d)], ("nlo", u, d), stage)

            for c in range(CH):
                pieces["stat", c] = lambda c=c: stat(c)
            pieces["aggregate"], pieces["scale"], pieces["bias"] = aggregate, scale, add_bias
            for d in range(KD):
                pieces["turn", d] = lambda d=d: turn(d)
            return pieces

        def layer_up(u, fc):
            def before(name, back):
                i = (NFC * u + fc) - back
                step = (name, i // NFC % 2, i % NFC)
                return ("prev", step) if i < 0 else step
            bank, held = up[fc % UP], act[fc % UP]

            def fn(e, it):
                for i, (d, (pw, px)) in enumerate((d, pr) for d in range(KD) for pr in PRODUCTS):
                    ins = e.matmul(bank[:, :], w1[pw][:, d, fc * P:(fc + 1) * P], nT[u][px][:, d, :],
                                   start=(i == 0), stop=(i == KD * len(PRODUCTS) - 1))
                return ins
            ready = ("nlo", u, KD - 1) if u else ("prev", ("nlo", u, KD - 1))
            ph.op("tensor", fn, [("prev", ("w1", "lo", SPLITS - 1)), ready, before("gelu", UP)], ("up", u, fc))
            ph.apart.add(("gelu", u, fc))
            ph.op("scalar", lambda e, it: e.activation(held[:, :], bank[:, :], ACT.Gelu_apprx_tanh,
                                                       bias=b1[:, bass.ds(it, 1), fc:fc + 1].rearrange("p o c -> p (o c)")),
                  [("up", u, fc), before("hlo", UP)], ("gelu", u, fc))
            free = ("down", 0, CH - 1) if u else ("prev", ("down", 1, CH - 1))
            if fc % 2:
                ph.op("scalar", lambda e, it: e.activation(hid[0][:, fc, :], held[:, :], ACT.Copy),
                      [("gelu", u, fc), free], ("hhi", u, fc))
            else:
                ph.op("vector", lambda e, it: e.tensor_copy(hid[0][:, fc, :], held[:, :]),
                      [("gelu", u, fc), free], ("hhi", u, fc))
            ph.op("vector", lambda e, it: e.tensor_tensor(hid[1][:, fc, :], held[:, :], hid[0][:, fc, :].bitcast(F32), ALU.subtract),
                  [("hhi", u, fc)], ("hlo", u, fc))

        def layer_down(u, c, chunks):
            bank = down[c % 2]
            for fc in chunks:
                def fn(e, it, fc=fc):
                    for i, (ph_, pw) in enumerate(PRODUCTS):
                        ins = e.matmul(bank[:, 0:D], hid[ph_][:, fc, c * P:(c + 1) * P], w2[pw][:, fc, :],
                                       start=(fc == 0 and i == 0), stop=(fc == NFC - 1 and i == len(PRODUCTS) - 1))
                    return ins
                after = []
                if fc == 0:
                    bank_before = ("y", u, c - 2) if c >= 2 else ("y", 0, c + 2) if u else ("prev", ("y", 1, c + 2))
                    after = [bank_before]
                if c == 0:
                    after += [("hlo", u, fc), ("w2", "lo", fc * SPLITS // NFC)]
                ph.op("tensor", fn, after, ("down", u, c) if fc == NFC - 1 else None)

        def finish(u, c):
            biased = ("bias", u) if u else ("prev", ("bias", u))
            ph.op("vector", lambda e, it: e.tensor_tensor(y[u][:, c, :], down[c % 2][:, 0:D], g[u][:, c, D:2 * D], ALU.add),
                  [("down", u, c), biased, ("prev", ("scatter", u, c))], ("y", u, c))
            ph.dma("gpsimd", [lambda e, it: e.indirect_dma_start(
                out=out, out_offset=bass.IndirectOffsetOnAxis(ap=rows[u][:, c:c + 1], axis=0),
                in_=y[u][:, c, :], in_offset=None)], [("y", u, c), ("rows", u)], ("scatter", u, c))
            gather(u, c)

        load_weights("w1", w1raw, a["w1"])
        load_weights("w2", w2raw, a["w2"])
        for u in range(U):
            load_bias(u)
        for u in range(U):
            pieces = prepare(1 - u)
            next_rows(u)
            for fc in range(NFC):
                layer_up(u, fc)
                if u == 0 and fc < SPLITS:
                    split_piece("w2", fc)
                if 2 <= fc < CH + 2:
                    pieces["stat", fc - 2]()
                if fc == CH + 1:
                    pieces["aggregate"]()
            pieces["scale"]()
            pieces["bias"]()
            layer_down(u, 0, range(NFC - 1))
            layer_down(u, 1, range(NFC - 1))
            for c in range(CH):
                layer_down(u, c, range(NFC) if c > 1 else [NFC - 1])
                finish(u, c)
                if u == 1:
                    for i in {0: [0], 1: [1], 2: [2, 3], 3: []}[c]:
                        split_piece("w1", i)
                if c == 1:
                    pieces["turn", 0]()
                    pieces["turn", 1]()
        run_phase(nc, ph, ["sync", "gpsimd", "vector", "scalar", "tensor"],
                  [(-1, {0}, {""}), (0, {0, 1}, {""}), ((1, E - 1), {0, 1}, {""}), (E - 1, {1}, {""})],
                  {"sync": load_constants, "scalar": lambda e: e.wait_ge(s_b1, 16)})
        with nc.Block() as block:
            @block.sync
            def _(e):
                for u in range(U):
                    for c in range(CH):
                        e.wait_ge(*ph.value(("scatter", u, c), E - 1))


def kernel(**inputs):
    import concourse.bacc as bacc
    from concourse.bass_utils import run_bass_kernel_spmd

    def on_partitions(w):
        return w.reshape(-1, P, w.shape[-1]).transpose(1, 0, 2)

    i = {n: np.asarray(v) for n, v in inputs.items()}
    row, col = np.arange(P)[:, None], np.arange(P)[None, :]
    shifts = [BITS * s for s in range(STEPS)][::-1]
    beyond = 0xff7fffff
    cand = np.array([[(c + 1) << s if (c + 1) << s < 2 ** 32 else beyond for c in range(CAND)] for s in shifts],
                    np.uint32).view(np.int32)
    arrays = {
        "x": i["L0_attn_x"],
        "wq": on_partitions(i["L0_attn_Wq"].T), "wk": on_partitions(i["L0_attn_Wk"].T),
        "wv": on_partitions(i["L0_attn_Wv"].T), "wo": on_partitions(i["L0_attn_Wo"].T),
        "qk_w": np.stack([np.tile(i["L0_attn_qn_w"], HU), np.tile(i["L0_attn_kn_w"], HU)], 1),
        "centroids": on_partitions(i["L0_ffn_centroids"].T),
        "ln_g": i["L0_ffn_ln_g"].reshape(KD, P).T, "ln_b": i["L0_ffn_ln_b"].reshape(KD, P).T,
        "w1": i["L0_ffn_w1"].reshape(E, KD, P, F).transpose(0, 2, 1, 3),
        "w2": i["L0_ffn_w2"].reshape(E, NFC, P, D).transpose(0, 2, 1, 3),
        "b1": i["L0_ffn_b1"].reshape(E, NFC, P).transpose(2, 0, 1),
        "b2": i["L0_ffn_b2"],
        "ident": np.eye(P, dtype=np.float32),
        "headsum": (row // DH == col // DH).astype(np.float32),
        "tokens": (np.arange(NT)[None, :] * P + np.arange(P)[:, None]).astype(np.int32),
        "cand_bits": np.broadcast_to(cand[None], (P, STEPS, CAND)),
        "steps_f": np.broadcast_to(np.array([2.0 ** s for s in shifts], np.float32)[None], (P, STEPS)),
    }
    nc = bacc.Bacc("TRN2", target_bir_lowering=False, num_devices=1)
    maps, aps = {}, {}
    for name, v in arrays.items():
        v = np.ascontiguousarray(v)
        maps[f"in_{name}"] = v
        aps[name] = nc.dram_tensor(f"in_{name}", v.shape, mybir.dt.from_np(v.dtype), kind="ExternalInput").ap()
    out = nc.dram_tensor("out", (T, D), F32, kind="ExternalOutput").ap()
    build(nc, aps, out)
    r = run_bass_kernel_spmd(nc, [maps], core_ids=[0])
    return r.results[0]["out"].reshape(B, N, D)
```
